# Optimizing a Trainium2 kernel written in Bass

```python
import numpy as np
import jax
import jax.numpy as jnp

def _softmax(x, axis=-1):
    return jax.nn.softmax(x, axis=axis)

def _gelu(x):
    return jax.nn.gelu(x, approximate=True)

def _silu(x):
    return jax.nn.silu(x)

def _sigmoid(x):
    return jax.nn.sigmoid(x)

def _layernorm(x, axis=-1, eps=1e-05):
    m = jnp.mean(x, axis=axis, keepdims=True)
    v = jnp.var(x, axis=axis, keepdims=True)
    return (x - m) / jnp.sqrt(v + eps)

def _scatter_add(tgt, idx, src, axis=0):
    return tgt.at[idx].add(src)

def _segment_sum(src, seg, n):
    return jax.ops.segment_sum(src, seg, n)
kernel_name = 'mk_adaln_attn_ffn_d1_seqx_r4_61bf44'

def setup_inputs(seed: int=0):
    np.random.seed(seed)
    _w = jnp.asarray

    def _rec_inputs():
        import jax
        import jax.numpy as jnp
        _rk = jax.random.key(seed)
        x = -0.0003929 + 0.9999 * jax.random.normal(jax.random.fold_in(_rk, 1), (32, 64, 256), jnp.float32)
        _lenS = 64 - jax.random.randint(jax.random.fold_in(_rk, 7), (32,), 0, max(1, 64 // 4) + 1, jnp.int32)
        _lenS2 = 64 - jax.random.randint(jax.random.fold_in(_rk, 8), (32,), 0, max(1, 64 // 4) + 1, jnp.int32)
        itok_B_0_7 = jax.random.randint(jax.random.fold_in(_rk, 11), (32,), 0, 8, jnp.int32)
        itok_B_0_8 = jax.random.randint(jax.random.fold_in(_rk, 12), (32,), 0, 9, jnp.int32)
        return (x, itok_B_0_7, itok_B_0_8)
    x, itok_B_0_7, itok_B_0_8 = _rec_inputs()

    def _L0_cond_setup():
        import jax, jax.numpy as jnp
        import numpy as np
        S, O, H = (8, 256, 256)
        B, N = (32, 128)
        key = jax.random.key(seed)
        k1, k2, k3, k4 = jax.random.split(key, 4)
        x = jax.random.normal(k1, (B, N, H), dtype=jnp.float32)
        subject_id = jax.random.randint(k2, (B,), 0, S)
        wbound = jnp.sqrt(2.0 / 6.0) * jnp.sqrt(3.0 / H)
        weight = jax.random.uniform(k3, (S, O, H), minval=-wbound, maxval=wbound, dtype=jnp.float32)
        bbound = 1.0 / jnp.sqrt(H)
        bias = jax.random.uniform(k4, (S, O), minval=-bbound, maxval=bbound, dtype=jnp.float32)
        return {'x': x, 'subject_id': subject_id, 'weight': weight, 'bias': bias}
    _L0_cond_all = _L0_cond_setup()
    _L0_cond_in = {k: v for k, v in _L0_cond_all.items() if k in ('weight', 'bias')}
    del _L0_cond_all

    def _L0_attn_setup():
        import jax, jax.numpy as jnp
        import numpy as np
        DIM = 256
        N_HEADS = 16
        HEAD_DIM = DIM // N_HEADS
        FREQS = [31.0, 37.0, 41.0, 43.0, 47.0]
        TWO_PI = 2.0 * float(np.pi)
        key = jax.random.key(seed)
        ks = jax.random.split(key, 16)
        B, L = (2, 256)
        s = 0.02
        inp = {'x': jax.random.normal(ks[0], (B, L, DIM), dtype=jnp.float32), 'Wq': jax.random.normal(ks[1], (DIM, DIM), dtype=jnp.float32) * s, 'bq': jnp.zeros((DIM,), dtype=jnp.float32), 'Wk': jax.random.normal(ks[2], (DIM, DIM), dtype=jnp.float32) * s, 'bk': jnp.zeros((DIM,), dtype=jnp.float32), 'Wv': jax.random.normal(ks[3], (DIM, DIM), dtype=jnp.float32) * s, 'bv': jnp.zeros((DIM,), dtype=jnp.float32), 'Wo': jax.random.normal(ks[4], (DIM, DIM), dtype=jnp.float32) * s, 'bo': jnp.zeros((DIM,), dtype=jnp.float32), 'alpha': jax.random.normal(ks[5], (N_HEADS, len(FREQS)), dtype=jnp.float32) * 0.1, 'phi': jax.random.uniform(ks[6], (N_HEADS, len(FREQS)), dtype=jnp.float32) * TWO_PI, 'temperature': jnp.ones((1,), dtype=jnp.float32), 'gamma': jnp.ones((DIM,), dtype=jnp.float32), 'beta': jnp.zeros((DIM,), dtype=jnp.float32)}
        return inp
    _L0_attn_all = _L0_attn_setup()
    _L0_attn_in = {k: v for k, v in _L0_attn_all.items() if k in ('Wq', 'bq', 'Wk', 'bk', 'Wv', 'bv', 'Wo', 'bo', 'alpha', 'phi', 'temperature', 'gamma', 'beta')}
    del _L0_attn_all

    def _L0_cond2_setup():
        import jax, jax.numpy as jnp
        import numpy as np
        LN_EPS = 1e-05
        key = jax.random.key(seed)
        ks = jax.random.split(key, 8)
        B, S, H, A, L = (32, 512, 256, 64, 10)
        return {'hidden_states': jax.random.normal(ks[0], (B, S, H), dtype=jnp.float32), 'language_ids': jax.random.randint(ks[1], (B,), 0, L, dtype=jnp.int64), 'W1': jax.random.normal(ks[2], (L, H, A), dtype=jnp.float32) * (1.0 / np.sqrt(H)), 'b1': jnp.zeros((L, A), dtype=jnp.float32), 'W2': jax.random.normal(ks[3], (L, A, H), dtype=jnp.float32) * (1.0 / np.sqrt(A)), 'b2': jnp.zeros((L, H), dtype=jnp.float32), 'gamma': jnp.ones((L, H), dtype=jnp.float32), 'beta': jnp.zeros((L, H), dtype=jnp.float32)}
    _L0_cond2_all = _L0_cond2_setup()
    _L0_cond2_in = {k: v for k, v in _L0_cond2_all.items() if k in ('W1', 'b1', 'W2', 'b2', 'gamma', 'beta')}
    del _L0_cond2_all

    def _L0_ffn_setup():
        import jax, jax.numpy as jnp
        import numpy as np
        from jax import lax
        T, B, I, M, O = (64, 64, 256, 256, 256)

        def _xavier(key, shape):
            fan_out, fan_in = shape
            limit = float(np.sqrt(6.0 / (fan_in + fan_out)))
            return jax.random.uniform(key, shape, jnp.float32, -limit, limit)
        key = jax.random.key(seed)
        ks = jax.random.split(key, 9)
        x = jax.random.normal(ks[0], (T, B, I), jnp.float32)
        return {'x': x, 'wf': _xavier(ks[1], (M, I)), 'uf': _xavier(ks[2], (M, M)), 'bf': jnp.zeros((M,), jnp.float32), 'wi': _xavier(ks[3], (M, I)), 'ui': _xavier(ks[4], (M, M)), 'bi': jnp.zeros((M,), jnp.float32), 'wc': _xavier(ks[5], (M, I)), 'uc': _xavier(ks[6], (M, M)), 'bc': jnp.zeros((M,), jnp.float32), 'wo': _xavier(ks[7], (O, I)), 'uo': _xavier(ks[8], (O, M)), 'bo': jnp.zeros((O,), jnp.float32), 'in_c': jnp.zeros((M,), jnp.float32)}
    _L0_ffn_all = _L0_ffn_setup()
    _L0_ffn_in = {k: v for k, v in _L0_ffn_all.items() if k in ('wf', 'uf', 'bf', 'wi', 'ui', 'bi', 'wc', 'uc', 'bc', 'wo', 'uo', 'bo', 'in_c')}
    del _L0_ffn_all
    return {'x': x, 'itok_B_0_7': itok_B_0_7, 'itok_B_0_8': itok_B_0_8, 'L0_cond_weight': _L0_cond_in['weight'], 'L0_cond_bias': _L0_cond_in['bias'], 'L0_attn_Wq': _L0_attn_in['Wq'], 'L0_attn_bq': _L0_attn_in['bq'], 'L0_attn_Wk': _L0_attn_in['Wk'], 'L0_attn_bk': _L0_attn_in['bk'], 'L0_attn_Wv': _L0_attn_in['Wv'], 'L0_attn_bv': _L0_attn_in['bv'], 'L0_attn_Wo': _L0_attn_in['Wo'], 'L0_attn_bo': _L0_attn_in['bo'], 'L0_attn_alpha': _L0_attn_in['alpha'], 'L0_attn_phi': _L0_attn_in['phi'], 'L0_attn_temperature': _L0_attn_in['temperature'], 'L0_attn_gamma': _L0_attn_in['gamma'], 'L0_attn_beta': _L0_attn_in['beta'], 'L0_cond2_W1': _L0_cond2_in['W1'], 'L0_cond2_b1': _L0_cond2_in['b1'], 'L0_cond2_W2': _L0_cond2_in['W2'], 'L0_cond2_b2': _L0_cond2_in['b2'], 'L0_cond2_gamma': _L0_cond2_in['gamma'], 'L0_cond2_beta': _L0_cond2_in['beta'], 'L0_ffn_wf': _L0_ffn_in['wf'], 'L0_ffn_uf': _L0_ffn_in['uf'], 'L0_ffn_bf': _L0_ffn_in['bf'], 'L0_ffn_wi': _L0_ffn_in['wi'], 'L0_ffn_ui': _L0_ffn_in['ui'], 'L0_ffn_bi': _L0_ffn_in['bi'], 'L0_ffn_wc': _L0_ffn_in['wc'], 'L0_ffn_uc': _L0_ffn_in['uc'], 'L0_ffn_bc': _L0_ffn_in['bc'], 'L0_ffn_wo': _L0_ffn_in['wo'], 'L0_ffn_uo': _L0_ffn_in['uo'], 'L0_ffn_bo': _L0_ffn_in['bo'], 'L0_ffn_in_c': _L0_ffn_in['in_c']}

def reference(x, itok_B_0_7, itok_B_0_8, L0_cond_weight, L0_cond_bias, L0_attn_Wq, L0_attn_bq, L0_attn_Wk, L0_attn_bk, L0_attn_Wv, L0_attn_bv, L0_attn_Wo, L0_attn_bo, L0_attn_alpha, L0_attn_phi, L0_attn_temperature, L0_attn_gamma, L0_attn_beta, L0_cond2_W1, L0_cond2_b1, L0_cond2_W2, L0_cond2_b2, L0_cond2_gamma, L0_cond2_beta, L0_ffn_wf, L0_ffn_uf, L0_ffn_bf, L0_ffn_wi, L0_ffn_ui, L0_ffn_bi, L0_ffn_wc, L0_ffn_uc, L0_ffn_bc, L0_ffn_wo, L0_ffn_uo, L0_ffn_bo, L0_ffn_in_c):
    import jax
    import jax.numpy as jnp

    def _L0_cond_ref(x, subject_id, weight, bias):
        import jax, jax.numpy as jnp
        import numpy as np
        S, O, H = (8, 256, 256)
        B, N = (32, 128)
        W = weight[subject_id]
        b = bias[subject_id]
        y = jnp.einsum('bnh,boh->bno', x, W) + b[:, None, :]
        return y

    def _L0_attn_ref(x, Wq, bq, Wk, bk, Wv, bv, Wo, bo, alpha, phi, temperature, gamma, beta):
        import jax, jax.numpy as jnp
        import numpy as np
        DIM = 256
        N_HEADS = 16
        HEAD_DIM = DIM // N_HEADS
        FREQS = [31.0, 37.0, 41.0, 43.0, 47.0]
        TWO_PI = 2.0 * float(np.pi)
        B, L, D = x.shape
        H, hd = (N_HEADS, HEAD_DIM)
        q = (x @ Wq.T + bq).reshape(B, L, H, hd).transpose(0, 2, 1, 3)
        k = (x @ Wk.T + bk).reshape(B, L, H, hd).transpose(0, 2, 1, 3)
        v = (x @ Wv.T + bv).reshape(B, L, H, hd).transpose(0, 2, 1, 3)
        sim = jnp.einsum('bhid,bhjd->bhij', q, k) / jnp.sqrt(jnp.asarray(hd, x.dtype))
        temp = jnp.abs(temperature)[0] + 0.1
        sim = sim / temp
        scores = jnp.zeros_like(sim)
        for fi, freq in enumerate(FREQS):
            a = alpha[:, fi][None, :, None, None]
            p = phi[:, fi][None, :, None, None]
            scores = scores + a * jnp.sin(TWO_PI * sim / freq + p)
        w = jax.nn.sigmoid(scores)
        w = w / (jnp.sum(w, axis=-1, keepdims=True) + 1e-10)
        out = jnp.einsum('bhij,bhjd->bhid', w, v)
        out = out.transpose(0, 2, 1, 3).reshape(B, L, D)
        out = out @ Wo.T + bo
        mu = jnp.mean(out, axis=-1, keepdims=True)
        var = jnp.mean(jnp.square(out - mu), axis=-1, keepdims=True)
        return (out - mu) / jnp.sqrt(var + 1e-05) * gamma + beta

    def _L0_cond2_ref(hidden_states, language_ids, W1, b1, W2, b2, gamma, beta):
        import jax, jax.numpy as jnp
        import numpy as np
        LN_EPS = 1e-05
        w1 = W1[language_ids]
        w2 = W2[language_ids]
        h = jnp.einsum('bsh,bha->bsa', hidden_states, w1) + b1[language_ids][:, None, :]
        h = jax.nn.relu(h)
        adapted = jnp.einsum('bsa,bah->bsh', h, w2) + b2[language_ids][:, None, :]
        x = hidden_states + adapted
        mean = jnp.mean(x, axis=-1, keepdims=True)
        var = jnp.mean(jnp.square(x - mean), axis=-1, keepdims=True)
        normed = (x - mean) * jax.lax.rsqrt(var + LN_EPS)
        return normed * gamma[language_ids][:, None, :] + beta[language_ids][:, None, :]

    def _L0_ffn_ref(x, wf, uf, bf, wi, ui, bi, wc, uc, bc, wo, uo, bo, in_c):
        import jax, jax.numpy as jnp
        import numpy as np
        from jax import lax
        T, B, I, M, O = (64, 64, 256, 256, 256)

        def _xavier(key, shape):
            fan_out, fan_in = shape
            limit = float(np.sqrt(6.0 / (fan_in + fan_out)))
            return jax.random.uniform(key, shape, jnp.float32, -limit, limit)
        batch = x.shape[1]
        c0 = jnp.broadcast_to(in_c, (batch, in_c.shape[0]))

        def step(c, xt):
            ft = jax.nn.sigmoid(xt @ wf.T + c @ uf.T + bf)
            it = jax.nn.sigmoid(xt @ wi.T + c @ ui.T + bi)
            gt = jnp.tanh(xt @ wc.T + c @ uc.T + bc)
            c = ft * c + it * gt
            return (c, None)
        c_final, _ = lax.scan(step, c0, x)
        h = jnp.tanh(jnp.einsum('tbi,oi->tbo', x, wo) + c_final @ uo.T + bo)
        return h
    x = x + _L0_attn_ref(_L0_cond_ref(x, itok_B_0_7, L0_cond_weight, L0_cond_bias), L0_attn_Wq, L0_attn_bq, L0_attn_Wk, L0_attn_bk, L0_attn_Wv, L0_attn_bv, L0_attn_Wo, L0_attn_bo, L0_attn_alpha, L0_attn_phi, L0_attn_temperature, L0_attn_gamma, L0_attn_beta)
    x = x + _L0_ffn_ref(_L0_cond2_ref(x, itok_B_0_8, L0_cond2_W1, L0_cond2_b1, L0_cond2_W2, L0_cond2_b2, L0_cond2_gamma, L0_cond2_beta), L0_ffn_wf, L0_ffn_uf, L0_ffn_bf, L0_ffn_wi, L0_ffn_ui, L0_ffn_bi, L0_ffn_wc, L0_ffn_uc, L0_ffn_bc, L0_ffn_wo, L0_ffn_uo, L0_ffn_bo, L0_ffn_in_c)
    return x

_drawn_inputs = setup_inputs


def setup_inputs(seed=0):
    import zlib

    import numpy as np

    out = dict(_drawn_inputs(seed))
    spreads = {'L0_attn_bq': (0.0, 2.0),
     'L0_attn_bk': (0.0, 2.0),
     'L0_attn_bv': (0.0, 0.1),
     'L0_attn_bo': (0.0, 0.1),
     'L0_attn_gamma': (1.0, 0.2),
     'L0_attn_beta': (0.0, 0.1),
     'L0_cond2_b1': (0.0, 0.38),
     'L0_cond2_b2': (0.0, 0.1),
     'L0_cond2_gamma': (1.0, 0.2),
     'L0_cond2_beta': (0.0, 0.1),
     'L0_ffn_bf': (0.0, 0.354),
     'L0_ffn_bi': (0.0, 0.438),
     'L0_ffn_bc': (0.0, 0.1),
     'L0_ffn_bo': (0.0, 0.1),
     'L0_ffn_in_c': (0.0, 2.0)}
    factors = {'L0_attn_Wq': 37.878, 'L0_attn_Wk': 33.647, 'L0_attn_alpha': 25.688, 'L0_attn_phi': 30.087}
    for name, (base, spread) in spreads.items():
        noise = np.random.default_rng([zlib.crc32(name.encode()), seed]).standard_normal(out[name].shape)
        drawn = base * np.exp(spread * noise) if base else spread * noise
        out[name] = jnp.asarray(drawn.astype(out[name].dtype))
    for name, factor in factors.items():
        out[name] = (out[name] * factor).astype(out[name].dtype)
    return out
```

```python
import math
from contextlib import ExitStack

import concourse.bass as bass
from concourse import mybir

P = 128
F32 = mybir.dt.float32
I32 = mybir.dt.int32
ALU = mybir.AluOpType
ACT = mybir.ActivationFunctionType

B, L, D = 32, 64, 256
KC = D // P
H, HD = 16, 16
GB = 8
NG = B // GB
NT = GB * L
BP = GB // 2
HC = H // KC
HQ = H // 4
HN = BP * L
A = 64
NF = 5
FREQS = (31.0, 37.0, 41.0, 43.0, 47.0)
NSUB, NLANG = 8, 10
EPS_LN, EPS_W = 1e-5, 1e-10
GATES = 3
WC_COLS = KC * D + KC
WA_COLS = KC * A + 3 * KC
W2_COLS = D + 1

TURN_BITS = 20
TURN = float(1 << TURN_BITS)
PI_LOW = 3.1415925
ROUND = 1.5 * 2.0 ** 23
TWO_PI_HI = 6.28125
TWO_PI_LO = 2 * math.pi - TWO_PI_HI

C_BQ, C_BK, C_BO, C_GAMMA, C_BETA, C_BOUT = 0, 2, 4, 6, 8, 10
C_TEMP, C_EPS = 12, 13
C_ALPHA = 14
C_PHI = C_ALPHA + H * NF
C_COLS = C_PHI + H * NF

DVE_LINKS = 24


def build(nc, x_in, ids_in, small_in, cond_in, down_in, up_in, wq_in, wk_in, wv_in, bv_in, wo_in,
          gate_w_in, gate_u_in, gate_b_in, c0_in, c0t_in, wout_in, uout_in, eye_in, out):
    with ExitStack() as ctx:
        def sb(name, shape, dt=F32):
            return ctx.enter_context(nc.sbuf_tensor(name, shape, dt))

        def pb(name, shape, dt=F32):
            return ctx.enter_context(nc.psum_tensor(name, shape, dt))

        def sem(name):
            return ctx.enter_context(nc.semaphore(name))

        ids = sb("ids", [1, 2 * B], I32)
        small = sb("small", [P, C_COLS])
        wq = sb("wq", [P, KC, D])
        wk = sb("wk", [P, KC, D])
        wv = sb("wv", [P, KC, D])
        bv = sb("bv", [P, D])
        wo = sb("wo", [P, 2, HQ, D])
        gate_w = sb("gate_w", [P, KC, 2, GATES * P])
        gate_u = sb("gate_u", [P, KC, 2, GATES * P])
        gate_b = sb("gate_b", [P, GATES * P])
        wout = sb("wout", [P, KC, D])
        uout = sb("uout", [P, KC, D])
        eye = sb("eye", [P, P])
        mean_w = sb("mean_w", [P, P])
        pair_ones = sb("pair_ones", [P, 32])
        qs = sb("qs", [P, 4])
        bqs = sb("bqs", [P, KC])
        phase = sb("phase", [P, H * NF])
        turns = sb("turns", [P, H * NF])
        xg = sb("xg", [P, KC, NT])
        wc = sb("wc", [P, GB, WC_COLS])
        wa = sb("wa", [P, GB, WA_COLS])
        w2 = sb("w2", [A, GB, W2_COLS])
        yT = sb("yT", [P, KC, NT])
        qT = sb("qT", [P, KC, NT])
        kT = sb("kT", [P, KC, NT])
        qm = sb("qm", [P, KC, GB, HC, L])
        vz = sb("vz", [P, BP, H, 32])
        sc = sb("sc", [P, H, BP, L])
        ang = sb("ang", [P, 2, NF, HN], I32)
        att = sb("att", [P, BP, HQ, L])
        rden = sb("rden", [P, HQ * L])
        oT = sb("oT", [P, KC, NT])
        sq = sb("sq", [P, KC, NT])
        rstd = sb("rstd", [P, NT])
        x1g = sb("x1g", [P, KC, NT])
        hT = sb("hT", [A, GB, L])
        zT = sb("zT", [P, KC, NT])
        x1_all = sb("x1_all", [P, NG, KC, NT])
        go_all = sb("go_all", [P, NG, KC, NT])
        cst = sb("cst", [P, P])
        cT = sb("cT", [P, KC, L])
        pre = sb("pre", [P, GATES * P])
        gat = sb("gat", [P, GATES * P])
        fc = sb("fc", [P, 2, P])
        hoc = rden[:, 0:KC * L].rearrange("p (c n) -> p c n", c=KC)

        pa = pb("pa", [P, KC, NT])
        pp = pb("pp", [P, KC, NT])
        ps = pb("ps", [P, 2, NT])
        pv = pb("pv", [P, 2, NT])

        const_in, x_in_s, ids_s = sem("const_in"), sem("x_loaded"), sem("ids_loaded")
        setup_pool, setup_dve = sem("setup_pool"), sem("setup_dve")
        wc_free, wc_loaded = sem("wc_free"), sem("wc_loaded")
        wa_free, wa_loaded = sem("wa_free"), sem("wa_loaded")
        x_free = sem("x_free")
        cond_done, y_ready = sem("cond_done"), sem("y_ready")
        q_done, q_ready = sem("q_done"), sem("q_ready")
        qm_loaded = [sem(f"qm_loaded{c}") for c in range(KC)]
        k_done, k_ready = sem("k_done"), sem("k_ready")
        v_done, v_ready = sem("v_done"), sem("v_ready")
        s_done, s_copied = sem("s_done"), sem("s_copied")
        angle_ready, sine_ready = sem("angle_ready"), sem("sine_ready")
        score_sum, score_ready, w_ready = sem("score_sum"), sem("score_ready"), sem("w_ready")
        pv_done, att_ready = sem("pv_done"), sem("att_ready")
        o_done, o_ready = sem("o_done"), sem("o_ready")
        mean_done, dev_ready, sq_ready = sem("mean_done"), sem("dev_ready"), sem("sq_ready")
        var_done, std_ready = sem("var_done"), sem("std_ready")
        x1_ready, x1_kept = sem("x1_ready"), sem("x1_kept")
        down_done, h_ready, up_done, x2_ready = sem("down_done"), sem("h_ready"), sem("up_done"), sem("x2_ready")
        z_ready, go_done, go_kept = sem("z_ready"), sem("go_done"), sem("go_kept")
        gate_done, pre_ready, gate_ready = sem("gate_done"), sem("pre_ready"), sem("gate_ready")
        c_ready, ct_done, ct_ready = sem("c_ready"), sem("ct_done"), sem("ct_ready")
        dve_link, setup_link = sem("dve_link"), sem("setup_link")
        angle_raw, cell = sem("angle_raw"), sem("cell")
        hoc_done, hoc_ready = sem("hoc_done"), sem("hoc_ready")
        tail_sum, tail_tanh, tail_out, stored = sem("tail_sum"), sem("tail_tanh"), sem("tail_out"), sem("stored")

        block = ctx.enter_context(nc.Block())
        N_CONST = 16

        def scal(col):
            return small[:, col:col + 1]

        @block.sync
        def _(sp):
            sp.dma_start(ids[:, :], ids_in).then_inc(ids_s, 16)
            loads = ((small, small_in), (wq, wq_in), (wk, wk_in), (wv, wv_in), (bv, bv_in), (wo, wo_in),
                     (gate_w, gate_w_in), (gate_u, gate_u_in), (gate_b, gate_b_in), (cst, c0_in),
                     (cT, c0t_in), (wout, wout_in), (uout, uout_in), (eye, eye_in))
            for dst, src in loads:
                sp.dma_start(dst[:], src).then_inc(const_in, 16)
            sp.wait_ge(ids_s, 16)
            with sp.Fori(0, NG) as g:
                sp.wait_ge(x_free, g + 1)
                sp.dma_start(xg[:], x_in[bass.ds(g, 1)].rearrange("a p c n -> p (a c) n")).then_inc(x_in_s, 16)
                sp.wait_ge(wc_free, g + 1)
                for b in range(GB):
                    s = sp.value_load(ids[0:1, bass.ds(g * GB + b, 1)], min_val=0, max_val=NSUB - 1)
                    sp.dma_start(wc[:, b, :], cond_in[bass.ds(s, 1)].rearrange("a p n -> p (a n)")).then_inc(wc_loaded, 16)
                sp.wait_ge(wa_free, g + 1)
                for b in range(GB):
                    s = sp.value_load(ids[0:1, bass.ds(g * GB + (B + b), 1)], min_val=0, max_val=NLANG - 1)
                    sp.dma_start(wa[:, b, :], down_in[bass.ds(s, 1)].rearrange("a p n -> p (a n)")).then_inc(wa_loaded, 16)
                    sp.dma_start(w2[:, b, :], up_in[bass.ds(s, 1)].rearrange("a p n -> p (a n)")).then_inc(wa_loaded, 16)
                sp.wait_ge(q_ready, g + 1)
                for c in range(KC):
                    for h in range(HC):
                        r = slice(HD * h, HD * h + HD)
                        sp.dma_start(qm[r, c, :, h, :], qT[r, c, :].rearrange("p (b n) -> p b n", b=GB)).then_inc(qm_loaded[c], 16)
            with sp.Fori(0, NG) as g:
                sp.wait_ge(tail_out, g + 1)
                sp.dma_start(out[bass.ds(g, 1)].rearrange("a p c n -> p (a c) n"),
                             go_all[:, bass.ds(g, 1), :, :].rearrange("p a c n -> p (a c) n")).then_inc(stored, 16)
            sp.wait_ge(stored, 16 * NG)

        @block.gpsimd
        def _(pool):
            pool.memset(vz[:], 0.0).then_inc(setup_pool, 1)
            pool.memset(qm[:], 0.0).then_inc(setup_pool, 1)
            pool.memset(mean_w[:], 1.0 / D).then_inc(setup_pool, 1)
            pool.memset(pair_ones[:], 0.0).then_inc(setup_pool, 1)
            pool.wait_ge(setup_pool, 4)
            pool.memset(pair_ones[0:L, 0:HD], 1.0).then_inc(setup_pool, 1)
            pool.memset(pair_ones[L:P, HD:2 * HD], 1.0).then_inc(setup_pool, 1)
            pool.wait_ge(setup_pool, 6)
            pool.sem_inc(x_free, 1)
            pool.sem_inc(wc_free, 1)
            pool.sem_inc(wa_free, 1)
            with pool.Fori(0, NG) as g:
                pool.wait_ge(x1_ready, g + 1)
                pool.tensor_copy(x1_all[:, bass.ds(g, 1), :, :].rearrange("p a c n -> p (a c n)"),
                                 x1g[:].rearrange("p c n -> p (c n)")).then_inc(x1_kept, 1)

        @block.tensor
        def _(pe):
            pe.wait_ge(const_in, 16 * 14)
            pe.wait_ge(setup_pool, 6)
            with pe.Fori(0, NG) as g:
                pe.wait_ge(x_in_s, g * 16 + 16)
                pe.wait_ge(wc_loaded, g * (16 * GB) + 16 * GB)
                for b in range(GB):
                    for oc in range(KC):
                        for kc in range(KC):
                            mm = pe.matmul(pa[:, oc, b * L:(b + 1) * L], wc[:, b, kc * D + oc * P:kc * D + (oc + 1) * P],
                                           xg[:, kc, b * L:(b + 1) * L], start=(kc == 0), stop=(kc == KC - 1))
                mm.then_inc(cond_done, 1)

                def project(dst, w, src):
                    for oc in range(KC):
                        for kc in range(KC):
                            mm = pe.matmul(dst[:, oc, :], w[:, kc, oc * P:(oc + 1) * P], src[:, kc, :],
                                           start=(kc == 0), stop=(kc == KC - 1))
                    return mm

                pe.wait_ge(y_ready, g + 1)
                project(pp, wq, yT).then_inc(q_done, 1)
                project(pa, wk, yT).then_inc(k_done, 1)
                pe.wait_ge(q_ready, g + 1)
                pvw = pp[:].rearrange("p c (u n) -> p (c u) n", u=2)
                for bp in range(BP):
                    for kc in range(KC):
                        mm = pe.matmul(pvw[:, bp, :], yT[:, kc, bp * P:(bp + 1) * P], wv[:, kc, :],
                                       start=(kc == 0), stop=(kc == KC - 1))
                mm.then_inc(v_done, 1)
                pe.wait_ge(k_ready, g + 1)
                for c in range(KC):
                    pe.wait_ge(qm_loaded[c], g * (16 * HC) + 16 * HC)
                    for bp in range(BP):
                        t = c * BP + bp
                        if t >= 2:
                            pe.wait_ge(s_copied, g * (KC * BP) + (t - 1))
                        for u in range(2):
                            b = 2 * bp + u
                            mm = pe.matmul(ps[u * L:(u + 1) * L, t % 2, :], kT[:, c, b * L:(b + 1) * L],
                                           qm[:, c, b, :, :], start=True, stop=True)
                        mm.then_inc(s_done, 1)
                pe.wait_ge(v_ready, g + 1)
                pe.wait_ge(w_ready, g * KC + KC)
                for bp in range(BP):
                    if bp >= 2:
                        pe.wait_ge(att_ready, g * BP + (bp - 1))
                    for h in range(H):
                        q, m = h // 4, h % 4
                        pe.matmul(pv[32 * m:32 * m + 32, bp % 2, q * L:(q + 1) * L], vz[:, bp, h, :], sc[:, h, bp, :],
                                  start=True, stop=True)
                    for m in range(4):
                        mm = pe.matmul(pv[32 * m:32 * m + 32, bp % 2, HQ * L:2 * HQ * L], pair_ones[:, :],
                                       sc[:, m:H:4, bp, :], start=True, stop=True)
                    mm.then_inc(pv_done, 1)
                pe.wait_ge(att_ready, g * BP + BP)
                for oc in range(KC):
                    po = pa[:, oc, :].rearrange("p (b u n) -> p b u n", u=2, n=L)
                    for u in range(2):
                        for q in range(HQ):
                            mm = pe.matmul(po[:, :, u, :], wo[:, u, q, oc * P:(oc + 1) * P], att[:, :, q, :],
                                           start=(q == 0), stop=(q == HQ - 1))
                mm.then_inc(o_done, 1)

                def average(dst, src):
                    for kc in range(KC):
                        mm = pe.matmul(dst, mean_w[:, :], src[:, kc, :], start=(kc == 0), stop=(kc == KC - 1))
                    return mm

                pe.wait_ge(o_ready, g + 1)
                average(pp[:, 0, :], oT).then_inc(mean_done, 1)
                pe.wait_ge(sq_ready, g * 2 + 1)
                average(pp[:, 1, :], sq).then_inc(var_done, 1)
                pe.wait_ge(x1_ready, g + 1)
                pe.wait_ge(wa_loaded, g * (32 * GB) + 32 * GB)
                for b in range(GB):
                    for kc in range(KC):
                        mm = pe.matmul(pa[0:A, 0, b * L:(b + 1) * L], wa[:, b, kc * A:(kc + 1) * A],
                                       x1g[:, kc, b * L:(b + 1) * L], start=(kc == 0), stop=(kc == KC - 1))
                mm.then_inc(down_done, 1)
                pe.wait_ge(h_ready, g + 1)
                for b in range(GB):
                    for oc in range(KC):
                        mm = pe.matmul(pp[:, oc, b * L:(b + 1) * L], w2[:, b, oc * P:(oc + 1) * P], hT[:, b, :],
                                       start=True, stop=True)
                mm.then_inc(up_done, 1)
                pe.wait_ge(x2_ready, g + 1)
                average(pa[:, 0, :], oT).then_inc(mean_done, 1)
                pe.wait_ge(sq_ready, g * 2 + 2)
                average(pa[:, 1, :], sq).then_inc(var_done, 1)
                pe.wait_ge(z_ready, g + 1)
                project(pp, wout, zT).then_inc(go_done, 1)
                pe.wait_ge(go_kept, g + 1)
                for t in range(GB):
                    for u in range(2):
                        for kc in range(KC):
                            pe.matmul(pv[u * L:(u + 1) * L, 1, 0:GATES * P], zT[:, kc, t * L:(t + 1) * L],
                                      gate_w[:, kc, u, :], start=(kc == 0), stop=False)
                    if t >= 1:
                        pe.wait_ge(ct_ready, g * GB + t)
                    for kc in range(KC):
                        for u in range(2):
                            mm = pe.matmul(pv[u * L:(u + 1) * L, 1, 0:GATES * P], cT[:, kc, :],
                                           gate_u[:, kc, u, :], start=False, stop=(kc == KC - 1))
                    mm.then_inc(gate_done, 1)
                    pe.wait_ge(c_ready, g * GB + (t + 1))
                    pe.transpose(pv[:, 0, 0:P], cst[:, :], eye[:, :]).then_inc(ct_done, 1)
                pe.wait_ge(ct_ready, g * GB + GB)
            for oc in range(KC):
                for kc in range(KC):
                    mm = pe.matmul(pa[:, oc, 0:L], uout[:, kc, oc * P:(oc + 1) * P], cT[:, kc, :],
                                   start=(kc == 0), stop=(kc == KC - 1))
            mm.then_inc(hoc_done, 1)

        @block.scalar
        def _(act):
            act.wait_ge(const_in, 16 * 14)
            act.wait_ge(setup_dve, 1)
            with act.Fori(0, NG) as g:
                act.wait_ge(q_done, g + 1)
                for c in range(KC):
                    op = act.activation(qT[:, c, :], pp[:, c, :], ACT.Identity, scale=qs[:, 0:1], bias=bqs[:, c:c + 1])
                op.then_inc(q_ready, 1)
                act.wait_ge(k_done, g + 1)
                for c in range(KC):
                    op = act.activation(kT[:, c, :], pa[:, c, :], ACT.Identity, bias=scal(C_BK + c))
                op.then_inc(k_ready, 1)
                for t in range(KC * BP):
                    c, bp = t // BP, t % BP
                    act.wait_ge(s_done, g * (KC * BP) + (t + 1))
                    act.activation(sc[:, c * HC:(c + 1) * HC, bp, :], ps[:, t % 2, :].rearrange("p (h n) -> p h n", h=HC),
                                   ACT.Copy).then_inc(s_copied, 1)
                for h in range(H):
                    act.wait_ge(angle_ready, g * H + (h + 1))
                    a = ang[:, h % 2, :, :].rearrange("p f n -> p (f n)")
                    act.activation(a.bitcast(F32), a, ACT.Sin, scale=2 * PI_LOW / TURN, bias=qs[:, 3:4]).then_inc(sine_ready, 1)
                for c in range(KC):
                    act.wait_ge(score_ready, g * H + HC * (c + 1))
                    w = sc[:, c * HC:(c + 1) * HC, :, :].rearrange("p h b n -> p (h b n)")
                    act.activation(w, w, ACT.Sigmoid).then_inc(w_ready, 1)
                act.wait_ge(o_done, g + 1)
                for c in range(KC):
                    op = act.activation(oT[:, c, :], pa[:, c, :], ACT.Identity, bias=scal(C_BO + c))
                op.then_inc(o_ready, 1)
                for n, pvar in enumerate((pp, pa)):
                    act.wait_ge(dev_ready, g * 2 + (n + 1))
                    act.activation(sq[:], oT[:], ACT.Square).then_inc(sq_ready, 1)
                    act.wait_ge(var_done, g * 2 + (n + 1))
                    act.activation(rstd[:, :], pvar[:, 1, :], ACT.Sqrt, bias=scal(C_EPS)).then_inc(std_ready, 1)
                act.wait_ge(go_done, g + 1)
                act.activation(go_all[:, bass.ds(g, 1), :, :].rearrange("p a c n -> p (a c n)"),
                               pp[:].rearrange("p c n -> p (c n)"), ACT.Copy).then_inc(go_kept, 1)
                for t in range(GB):
                    act.wait_ge(pre_ready, g * GB + (t + 1))
                    act.activation(gat[:, 0:2 * P], pre[:, 0:2 * P], ACT.Sigmoid).then_inc(gate_ready, 1)
                    act.activation(gat[:, 2 * P:3 * P], pre[:, 2 * P:3 * P], ACT.Tanh).then_inc(gate_ready, 1)
            act.wait_ge(hoc_done, 1)
            for c in range(KC):
                act.activation(hoc[:, c, :], pa[:, c, 0:L], ACT.Identity, bias=scal(C_BOUT + c)).then_inc(hoc_ready, 1)
            with act.Fori(0, NG) as g:
                act.wait_ge(tail_sum, g * KC + KC)
                go = go_all[:, bass.ds(g, 1), :, :].rearrange("p a c n -> p (a c n)")
                act.activation(go, go, ACT.Tanh).then_inc(tail_tanh, 1)

        @block.vector
        def _(dve):
            dve.wait_ge(const_in, 16 * 14)
            done = [0]

            def step(ins):
                done[0] += 1
                ins.then_inc(setup_link, 1)
                dve.wait_ge(setup_link, done[0])

            step(dve.scalar_tensor_tensor(out=qs[:, 1:2], in0=scal(C_TEMP), scalar=-1.0, in1=scal(C_TEMP), op0=ALU.mult,
                                          op1=ALU.max))
            step(dve.tensor_scalar(qs[:, 1:2], qs[:, 1:2], 0.1, None, ALU.add))
            step(dve.reciprocal(qs[:, 2:3], qs[:, 1:2]))
            step(dve.tensor_scalar(qs[:, 0:1], qs[:, 2:3], 1.0 / math.sqrt(HD), None, ALU.mult))
            step(dve.memset(qs[:, 3:4], -PI_LOW))
            step(dve.tensor_scalar(bqs[:, :], small[:, C_BQ:C_BQ + KC], qs[:, 0:1], None, ALU.mult))
            phi = small[:, C_PHI:C_PHI + H * NF]
            step(dve.tensor_scalar(turns[:, :], phi, 1 / (2 * math.pi), ROUND, ALU.mult, ALU.add))
            step(dve.tensor_scalar(turns[:, :], turns[:, :], ROUND, None, ALU.subtract))
            step(dve.scalar_tensor_tensor(out=phase[:, :], in0=turns[:, :], scalar=-TWO_PI_HI, in1=phi,
                                          op0=ALU.mult, op1=ALU.add))
            step(dve.scalar_tensor_tensor(out=phase[:, :], in0=turns[:, :], scalar=-TWO_PI_LO, in1=phase[:, :],
                                          op0=ALU.mult, op1=ALU.add))
            dve.tensor_scalar(phase[:, :], phase[:, :], TURN / (2 * math.pi), TURN / 2, ALU.mult,
                              ALU.add).then_inc(setup_dve, 1)
            dve.wait_ge(setup_dve, 1)
            dve.wait_ge(setup_pool, 6)

            with dve.Fori(0, NG) as g:
                links = [0]

                def link(ins):
                    links[0] += 1
                    ins.then_inc(dve_link, 1)
                    dve.wait_ge(dve_link, g * DVE_LINKS + links[0])

                def per_batch(tile, col, c=None):
                    return tile[:, :, col:col + 1].to_broadcast([P, GB, L])

                def by_batch(ap):
                    return ap.rearrange("p (b n) -> p b n", b=GB)

                dve.wait_ge(cond_done, g + 1)
                for c in range(KC):
                    op = dve.tensor_tensor(by_batch(yT[:, c, :]), by_batch(pa[:, c, :]), per_batch(wc, KC * D + c), ALU.add)
                op.then_inc(y_ready, 1)
                dve.wait_ge(y_ready, g + 1)
                dve.wait_ge(v_done, g + 1)
                vw = pp[:].rearrange("p c (u h d) -> p (c u) h d", u=2, d=HD)
                for u in range(2):
                    r = slice(u * L, (u + 1) * L)
                    bias = bv[r, :].rearrange("p (o h d) -> p o h d", o=1, d=HD).to_broadcast([L, BP, H, HD])
                    op = dve.tensor_tensor(vz[r, :, :, u * HD:(u + 1) * HD], vw[r], bias, ALU.add)
                op.then_inc(v_ready, 1)

                def head(h):
                    return sc[:, h, :, :].rearrange("p b n -> p (b n)")

                def angle(h, f):
                    dve.tensor_scalar(ang[:, h % 2, f, :], head(h), TURN / FREQS[f],
                                      phase[:, h * NF + f:h * NF + f + 1], ALU.mult, ALU.add).then_inc(angle_raw, 1)

                def wrap(h):
                    dve.wait_ge(angle_raw, g * (H * NF) + NF * (h + 1))
                    a = ang[:, h % 2, :, :].rearrange("p f n -> p (f n)")
                    dve.tensor_scalar(a, a, (1 << TURN_BITS) - 1, None, ALU.bitwise_and).then_inc(angle_ready, 1)

                def add_sine(h, f):
                    amp = scal(C_ALPHA + h * NF + f)
                    sine = ang[:, h % 2, f, :].bitcast(F32)
                    if f == 0:
                        dve.wait_ge(sine_ready, g * H + (h + 1))
                        dve.tensor_scalar(head(h), sine, amp, None, ALU.mult).then_inc(score_sum, 1)
                        return
                    dve.wait_ge(score_sum, g * (H * (NF - 1)) + h * (NF - 1) + f)
                    op = dve.scalar_tensor_tensor(out=head(h), in0=sine, scalar=amp, in1=head(h), op0=ALU.mult, op1=ALU.add)
                    op.then_inc(score_ready if f == NF - 1 else score_sum, 1)

                dve.wait_ge(s_copied, g * (KC * BP) + BP)
                for f in range(NF):
                    angle(0, f)
                wrap(0)
                for h in range(H):
                    if h + 1 == HC:
                        dve.wait_ge(s_copied, g * (KC * BP) + KC * BP)
                    if h >= 1:
                        dve.wait_ge(score_ready, g * H + h)
                    for f in range(NF):
                        if h + 1 < H:
                            angle(h + 1, f)
                    if h + 1 < H:
                        wrap(h + 1)
                    for f in range(NF):
                        add_sine(h, f)

                for bp in range(BP):
                    dve.wait_ge(pv_done, g * BP + (bp + 1))
                    link(dve.tensor_scalar(rden[:, :], pv[:, bp % 2, HQ * L:2 * HQ * L], EPS_W, None, ALU.add))
                    link(dve.reciprocal(rden[:, :], rden[:, :]))
                    dve.tensor_tensor(att[:, bp, :, :].rearrange("p q n -> p (q n)"), pv[:, bp % 2, 0:HQ * L], rden[:, :],
                                      ALU.mult).then_inc(att_ready, 1)
                    dve.wait_ge(att_ready, g * BP + (bp + 1))

                def normalise(n, pm):
                    dve.wait_ge(mean_done, g * 2 + (n + 1))
                    for c in range(KC):
                        op = dve.tensor_tensor(oT[:, c, :], oT[:, c, :], pm[:, 0, :], ALU.subtract)
                        if c == 0:
                            link(op)
                    op.then_inc(dev_ready, 1)
                    dve.wait_ge(dev_ready, g * 2 + (n + 1))
                    dve.wait_ge(std_ready, g * 2 + (n + 1))
                    link(dve.reciprocal(rstd[:, :], rstd[:, :]))

                dve.wait_ge(o_ready, g + 1)
                normalise(0, pp)
                for c in range(KC):
                    link(dve.scalar_tensor_tensor(out=oT[:, c, :], in0=oT[:, c, :], scalar=scal(C_GAMMA + c), in1=rstd[:, :],
                                                  op0=ALU.mult, op1=ALU.mult))
                for c in range(KC):
                    op = dve.scalar_tensor_tensor(out=x1g[:, c, :], in0=oT[:, c, :], scalar=scal(C_BETA + c),
                                                  in1=xg[:, c, :], op0=ALU.add, op1=ALU.add)
                    if c == 0:
                        link(op)
                op.then_inc(x1_ready, 1)
                dve.wait_ge(x1_ready, g + 1)
                dve.wait_ge(down_done, g + 1)
                link(dve.tensor_tensor(hT[:], by_batch(pa[0:A, 0, :]), w2[:, :, D:D + 1].to_broadcast([A, GB, L]), ALU.add))
                dve.tensor_scalar(hT[:], hT[:], 0.0, None, ALU.max).then_inc(h_ready, 1)
                dve.wait_ge(up_done, g + 1)
                for c in range(KC):
                    link(dve.tensor_tensor(oT[:, c, :], x1g[:, c, :], pp[:, c, :], ALU.add))
                for c in range(KC):
                    op = dve.tensor_tensor(by_batch(oT[:, c, :]), by_batch(oT[:, c, :]), per_batch(wa, KC * A + c), ALU.add)
                    if c == 0:
                        link(op)
                op.then_inc(x2_ready, 1)
                dve.wait_ge(x2_ready, g + 1)
                normalise(1, pa)
                for c in range(KC):
                    link(dve.tensor_tensor(oT[:, c, :], oT[:, c, :], rstd[:, :], ALU.mult))
                for c in range(KC):
                    link(dve.tensor_tensor(by_batch(oT[:, c, :]), by_batch(oT[:, c, :]), per_batch(wa, KC * A + KC + c), ALU.mult))
                for c in range(KC):
                    op = dve.tensor_tensor(by_batch(zT[:, c, :]), by_batch(oT[:, c, :]), per_batch(wa, KC * A + 2 * KC + c), ALU.add)
                    if c == 0:
                        link(op)
                op.then_inc(z_ready, 1)
                dve.wait_ge(z_ready, g + 1)
                dve.wait_ge(x1_kept, g + 1)
                dve.sem_inc(wa_free, 1)
                dve.sem_inc(wc_free, 1)
                dve.sem_inc(x_free, 1)

                for t in range(GB):
                    dve.wait_ge(gate_done, g * GB + (t + 1))
                    dve.tensor_tensor(pre[:, :], pv[:, 1, 0:GATES * P], gate_b[:, :], ALU.add).then_inc(pre_ready, 1)
                    dve.wait_ge(gate_ready, g * (2 * GB) + (2 * t + 1))
                    dve.tensor_tensor(fc[:, 0, :], gat[:, 0:P], cst[:, :], ALU.mult).then_inc(cell, 1)
                    dve.wait_ge(gate_ready, g * (2 * GB) + (2 * t + 2))
                    dve.tensor_tensor(fc[:, 1, :], gat[:, P:2 * P], gat[:, 2 * P:3 * P], ALU.mult).then_inc(cell, 1)
                    dve.wait_ge(cell, g * (2 * GB) + (2 * t + 2))
                    dve.tensor_tensor(cst[:, :], fc[:, 0, :], fc[:, 1, :], ALU.add).then_inc(c_ready, 1)
                    dve.wait_ge(ct_done, g * GB + (t + 1))
                    dve.tensor_copy(cT[:].rearrange("p c n -> p (c n)"), pv[:, 0, 0:P]).then_inc(ct_ready, 1)
                assert links[0] == DVE_LINKS, links[0]

            dve.wait_ge(hoc_ready, KC)
            with dve.Fori(0, NG) as g:
                for c in range(KC):
                    go = go_all[:, bass.ds(g, 1), c, :].rearrange("p a (t n) -> p (a t) n", n=L)
                    dve.tensor_tensor(go, go, hoc[:, c:c + 1, :].to_broadcast([P, GB, L]), ALU.add).then_inc(tail_sum, 1)
                dve.wait_ge(tail_tanh, g + 1)
                go = go_all[:, bass.ds(g, 1), :, :].rearrange("p a c n -> p (a c n)")
                x1 = x1_all[:, bass.ds(g, 1), :, :].rearrange("p a c n -> p (a c n)")
                dve.tensor_tensor(go, go, x1, ALU.add).then_inc(tail_out, 1)


_OUT = (NG, P, KC, NT)


def kernel(**inputs):
    import numpy as np
    import concourse.bacc as bacc
    from concourse.bass_utils import run_bass_kernel_spmd

    a = {k: np.asarray(v) for k, v in inputs.items()}

    def chunked(w):
        o, i = w.shape
        return w.T.reshape(i // P, P, o).transpose(1, 0, 2)

    def cols(v):
        return v.reshape(KC, P).T

    x = a["x"].reshape(NG, NT, KC, P).transpose(0, 3, 2, 1)
    ids = np.concatenate([a["itok_B_0_7"], a["itok_B_0_8"]]).reshape(1, 2 * B)
    rows = np.concatenate([a["L0_attn_temperature"], np.full(1, EPS_LN, np.float32), a["L0_attn_alpha"].reshape(-1),
                           a["L0_attn_phi"].reshape(-1)])
    small = np.concatenate([cols(a["L0_attn_bq"]), cols(a["L0_attn_bk"]), cols(a["L0_attn_bo"]), cols(a["L0_attn_gamma"]),
                            cols(a["L0_attn_beta"]), cols(a["L0_ffn_bo"]), np.broadcast_to(rows, (P, rows.size))], axis=1)
    cond = a["L0_cond_weight"].transpose(0, 2, 1).reshape(NSUB, KC, P, D).transpose(0, 2, 1, 3).reshape(NSUB, P, KC * D)
    cond = np.concatenate([cond, a["L0_cond_bias"].reshape(NSUB, KC, P).transpose(0, 2, 1)], axis=2)
    down = a["L0_cond2_W1"].reshape(NLANG, KC, P, A).transpose(0, 2, 1, 3).reshape(NLANG, P, KC * A)
    down = np.concatenate([down] + [a["L0_cond2_" + n].reshape(NLANG, KC, P).transpose(0, 2, 1) for n in ("b2", "gamma", "beta")], axis=2)
    up = np.concatenate([a["L0_cond2_W2"], a["L0_cond2_b1"][:, :, None]], axis=2)
    wo_t = a["L0_attn_Wo"].T.reshape(HQ, 4, HD, D).transpose(1, 2, 0, 3)
    wo = np.zeros((4, 2, HD, 2, HQ, D), np.float32)
    for u in range(2):
        wo[:, u, :, u] = wo_t
    wo = wo.reshape(P, 2, HQ, D)

    def gate_cols(ws):
        w = np.stack([chunked(w).reshape(P, KC, 2, P) for w in ws], axis=3)
        return w.reshape(P, KC, 2, GATES * P)

    gate_b = np.stack([a["L0_ffn_" + n].reshape(2, P) for n in ("bf", "bi", "bc")], axis=1).reshape(2, 1, GATES * P)
    arrays = {
        "x": x, "ids": ids, "small": small, "cond": cond, "down": down, "up": up,
        "wq": chunked(a["L0_attn_Wq"]), "wk": chunked(a["L0_attn_Wk"]), "wv": chunked(a["L0_attn_Wv"]),
        "bv": np.broadcast_to(a["L0_attn_bv"], (P, D)), "wo": wo,
        "gate_w": gate_cols([a["L0_ffn_" + n] for n in ("wf", "wi", "wc")]),
        "gate_u": gate_cols([a["L0_ffn_" + n] for n in ("uf", "ui", "uc")]),
        "gate_b": np.broadcast_to(gate_b, (2, L, GATES * P)).reshape(P, GATES * P),
        "c0": np.broadcast_to(a["L0_ffn_in_c"].reshape(2, 1, P), (2, L, P)).reshape(P, P),
        "c0t": np.broadcast_to(cols(a["L0_ffn_in_c"])[:, :, None], (P, KC, L)),
        "wout": chunked(a["L0_ffn_wo"]), "uout": chunked(a["L0_ffn_uo"]), "eye": np.eye(P, dtype=np.float32),
    }
    nc = bacc.Bacc("TRN2", target_bir_lowering=False, num_devices=1)
    feeds, args = {}, []
    for name, v in arrays.items():
        v = np.ascontiguousarray(v)
        feeds[f"in_{name}"] = v
        args.append(nc.dram_tensor(f"in_{name}", v.shape, mybir.dt.from_np(v.dtype), kind="ExternalInput").ap())
    args.append(nc.dram_tensor("out_t", _OUT, F32, kind="ExternalOutput").ap())
    build(nc, *args)
    r = run_bass_kernel_spmd(nc, [feeds], core_ids=[0])
    got = r.results[0]["out_t"]
    return got.transpose(0, 3, 2, 1).reshape(B, L, D)
```

```python
import math
from contextlib import ExitStack

import concourse.bass as bass
from concourse import mybir

P = 128
F32 = mybir.dt.float32
I32 = mybir.dt.int32
ALU = mybir.AluOpType
ACT = mybir.ActivationFunctionType

B, L, D = 32, 64, 256
KC = D // P
H, HD = 16, 16
GB = 8
NG = B // GB
NT = GB * L
HC = H // KC
NP = H // 2
PC = NP // KC
TB = 2
TC = GB // TB
NTILE = KC * TC
A = 64
NF = 5
FREQS = (31.0, 37.0, 41.0, 43.0, 47.0)
NSUB, NLANG = 8, 10
EPS_LN, EPS_W = 1e-5, 1e-10
GATES = 3
WC_COLS = KC * D + KC
WA_COLS = KC * A + 3 * KC
W2_COLS = D + 1

TURN_BITS = 20
TURN = float(1 << TURN_BITS)
PI_LOW = 3.1415925
ROUND = 1.5 * 2.0 ** 23
TWO_PI_HI = 6.28125
TWO_PI_LO = 2 * math.pi - TWO_PI_HI

C_BQ, C_BK, C_BO, C_GAMMA, C_BETA, C_BOUT = 0, 2, 4, 6, 8, 10
C_TEMP, C_EPS = 12, 13
C_ALPHA = 14
C_PHI = C_ALPHA + NP * NF
C_COLS = C_PHI + NP * NF

LINKS = 11
STEP_SLOT = NP - GB // 2


def wait(eng, sem, value):
    if not (isinstance(value, int) and value <= 0):
        eng.wait_ge(sem, value)


def build(nc, x_in, ids_in, small_in, cond_in, down_in, up_in, wq_in, wk_in, wv_in, bv_in, wo_in,
          gate_w_in, gate_u_in, gate_b_in, c0_in, c0t_in, wout_in, uout_in, eye_in, out):
    with ExitStack() as ctx:
        def sb(name, shape, dt=F32):
            return ctx.enter_context(nc.sbuf_tensor(name, shape, dt))

        def pb(name, shape, dt=F32):
            return ctx.enter_context(nc.psum_tensor(name, shape, dt))

        def sem(name):
            return ctx.enter_context(nc.semaphore(name))

        ids = sb("ids", [1, 2 * B], I32)
        small = sb("small", [P, C_COLS])
        wq = sb("wq", [P, KC, D])
        wk = sb("wk", [P, KC, D])
        wv = sb("wv", [P, KC, 2, P])
        bv = sb("bv", [P, P])
        wo = sb("wo", [P, KC, D])
        gate_w = sb("gate_w", [P, KC, 2, GATES * P])
        gate_u = sb("gate_u", [P, KC, 2, GATES * P])
        gate_b = sb("gate_b", [P, GATES * P])
        wout = sb("wout", [P, KC, D])
        uout = sb("uout", [P, KC, D])
        eye = sb("eye", [P, P])
        mean_w = sb("mean_w", [P, P])
        pair_ones = sb("pair_ones", [P, 32])
        qs = sb("qs", [P, 4])
        bqs = sb("bqs", [P, KC])
        phase = sb("phase", [P, NP * NF])
        turns = sb("turns", [P, NP * NF])
        xg = sb("xg", [P, KC, NT])
        wc = sb("wc", [P, GB, WC_COLS])
        yT = sb("yT", [P, KC, NT])
        qT = sb("qT", [P, KC, NT])
        kT = sb("kT", [P, KC, NT])
        qm = sb("qm", [P, KC, GB, 2, PC, L])
        vz = sb("vz", [P, GB, NP, 32])
        sc = sb("sc", [P, NP, GB, L])
        ang = sb("ang", [P, 2, NF, NT], I32)
        att = sb("att", [P, KC, NT])
        rden = sb("rden", [P, NT])
        xr = sb("xr", [P, KC, NT])
        wa = sb("wa", [P, GB, WA_COLS])
        w2 = sb("w2", [A, GB, W2_COLS])
        oT = sb("oT", [P, KC, NT])
        sq = sb("sq", [P, KC, NT])
        rstd = sb("rstd", [P, NT])
        x1g = sb("x1g", [P, KC, NT])
        hT = sb("hT", [A, GB, L])
        zT = sb("zT", [P, KC, NT])
        x1_dram = nc.dram_tensor("x1_kept", (NG, P, KC, NT), F32, kind="Internal").ap()
        x1_all = qm[:].rearrange("p c b u k n -> p (c b u k n)").rearrange("p (o g n) -> p o g n", o=2, g=NG)[:, 0]
        go_all = sb("go_all", [P, NG, KC, NT])
        cst = sb("cst", [P, P])
        cT = sb("cT", [P, KC, L])
        pre = sb("pre", [P, GATES * P])
        gat = sb("gat", [P, GATES * P])
        fc = sb("fc", [P, 2, P])
        hoc = sb("hoc", [P, KC, L])

        pf = pb("pf", [P, KC, NT])
        pr = pb("pr", [P, KC, NT])
        ps = pb("ps", [P, NT])
        pnum = pb("pnum", [P, NT])
        pden = pb("pden", [P, NT])
        pgate = pb("pgate", [P, NT])[:, 0:GATES * P]
        pct = pr[:, 1, 0:P]

        const_in, ids_s, setup_pool, setup_dve = sem("const_in"), sem("ids_loaded"), sem("setup_pool"), sem("setup_dve")
        setup_link, rest_link = sem("setup_link"), sem("rest_link")
        x_loaded, wc_loaded, xr_loaded, wa_loaded = sem("x_loaded"), sem("wc_loaded"), sem("xr_loaded"), sem("wa_loaded")
        rest_free = sem("rest_free")
        cond_done, y_ready, q_done, q_ready = sem("cond_done"), sem("y_ready"), sem("q_done"), sem("q_ready")
        qm_loaded = [sem(f"qm_loaded{c}") for c in range(KC)]
        k_done, k_ready, v_done, v_ready = sem("k_done"), sem("k_ready"), sem("v_done"), sem("v_ready")
        s_done, s_copied = sem("s_done"), sem("s_copied")
        angle_raw, angle_ready, sine_ready = sem("angle_raw"), sem("angle_ready"), sem("sine_ready")
        score_part, score_ready, w_ready = sem("score_part"), sem("score_ready"), sem("w_ready")
        pv_done, att_part, att_ready = sem("pv_done"), sem("att_part"), sem("att_ready")
        o_done, o_ready = sem("o_done"), sem("o_ready")
        mean_done, dev_ready, sq_ready = sem("mean_done"), sem("dev_ready"), sem("sq_ready")
        var_done, std_ready = sem("var_done"), sem("std_ready")
        x1_ready, x1_kept, down_done, h_ready = sem("x1_ready"), sem("x1_kept"), sem("down_done"), sem("h_ready")
        up_done, x2_ready, z_ready = sem("up_done"), sem("x2_ready"), sem("z_ready")
        go_done, go_kept = sem("go_done"), sem("go_kept")
        gate_done, pre_ready, gate_ready, cell = sem("gate_done"), sem("pre_ready"), sem("gate_ready"), sem("cell")
        c_ready, ct_done, ct_ready = sem("c_ready"), sem("ct_done"), sem("ct_ready")
        x1_loaded = sem("x1_loaded")
        hoc_done, hoc_ready = sem("hoc_done"), sem("hoc_ready")
        tail_sum, tail_tanh, tail_out, stored = sem("tail_sum"), sem("tail_tanh"), sem("tail_out"), sem("stored")

        consts = ((small, small_in), (wq, wq_in), (wk, wk_in), (wv, wv_in), (bv, bv_in), (wo, wo_in),
                  (gate_w, gate_w_in), (gate_u, gate_u_in), (gate_b, gate_b_in), (cst, c0_in),
                  (cT, c0t_in), (wout, wout_in), (uout, uout_in), (eye, eye_in))
        CONST_IN = 16 * len(consts)
        block = ctx.enter_context(nc.Block())

        def scal(col):
            return small[:, col:col + 1]

        def by_batch(ap):
            return ap.rearrange("p (b n) -> p b n", b=GB)

        def rounds(eng, step, first=True):
            if first:
                step(0, rest=False, attention=True, front=True)
            with eng.Fori(1, NG - 1) as i:
                step(i, rest=True, attention=True, front=True)
            step(NG - 1, rest=True, attention=True, front=False)
            step(NG, rest=True, attention=False, front=False)

        @block.sync
        def _(sp):
            def load_front(g):
                sp.dma_start(xg[:], x_in[bass.ds(g, 1)].rearrange("a p c n -> p (a c) n")).then_inc(x_loaded, 16)
                for b in range(GB):
                    s = sp.value_load(ids[0:1, bass.ds(g * GB + b, 1)], min_val=0, max_val=NSUB - 1)
                    sp.dma_start(wc[:, b, :], cond_in[bass.ds(s, 1)].rearrange("a p n -> p (a n)")).then_inc(wc_loaded, 16)

            def load_rest(g):
                sp.dma_start(xr[:], x_in[bass.ds(g, 1)].rearrange("a p c n -> p (a c) n")).then_inc(xr_loaded, 16)
                for b in range(GB):
                    s = sp.value_load(ids[0:1, bass.ds(g * GB + (B + b), 1)], min_val=0, max_val=NLANG - 1)
                    sp.dma_start(wa[:, b, :], down_in[bass.ds(s, 1)].rearrange("a p n -> p (a n)")).then_inc(wa_loaded, 16)
                    sp.dma_start(w2[:, b, :], up_in[bass.ds(s, 1)].rearrange("a p n -> p (a n)")).then_inc(wa_loaded, 16)

            def spread_q(g):
                sp.wait_ge(q_ready, g + 1)
                for c in range(KC):
                    for h in range(HC):
                        r = slice(HD * h, HD * h + HD)
                        sp.dma_start(qm[r, c, :, h % 2, h // 2, :], by_batch(qT[r, c, :])).then_inc(qm_loaded[c], 16)

            sp.dma_start(ids[:, :], ids_in).then_inc(ids_s, 16)
            sp.wait_ge(ids_s, 16)
            load_front(0)
            for dst, src in consts:
                sp.dma_start(dst[:], src).then_inc(const_in, 16)
            sp.wait_ge(setup_pool, 6)
            spread_q(0)

            def step(i, rest, attention, front):
                if front:
                    sp.wait_ge(y_ready, i + 1)
                    load_front(i + 1)
                if rest:
                    sp.wait_ge(rest_free, i)
                    load_rest(i - 1)
                if front:
                    spread_q(i + 1)

            rounds(sp, step)
            sp.wait_ge(s_done, NG * NTILE)
            sp.wait_ge(x1_kept, 16 * NG)
            sp.dma_start(x1_all.rearrange("p g (c n) -> p g c n", c=KC), x1_dram.rearrange("g p c n -> p g c n")).then_inc(x1_loaded, 16)
            with sp.Fori(0, NG) as g:
                sp.wait_ge(tail_out, g + 1)
                sp.dma_start(out[bass.ds(g, 1)].rearrange("a p c n -> p (a c) n"),
                             go_all[:, bass.ds(g, 1), :, :].rearrange("p a c n -> p (a c) n")).then_inc(stored, 16)
            sp.wait_ge(stored, 16 * NG)

        @block.gpsimd
        def _(pool):
            pool.memset(qm[:], 0.0).then_inc(setup_pool, 1)
            pool.memset(mean_w[:], 1.0 / D).then_inc(setup_pool, 1)
            pool.memset(pair_ones[:], 0.0).then_inc(setup_pool, 1)
            pool.memset(vz[:], 0.0).then_inc(setup_pool, 1)
            pool.wait_ge(setup_pool, 4)
            pool.memset(pair_ones[0:L, 0:HD], 1.0).then_inc(setup_pool, 1)
            pool.memset(pair_ones[L:P, HD:2 * HD], 1.0).then_inc(setup_pool, 1)
            pool.wait_ge(setup_pool, 6)
            pool.sem_inc(rest_free, 1)
            with pool.Fori(0, NG) as g:
                pool.wait_ge(x1_ready, g + 1)
                pool.dma_start(x1_dram[bass.ds(g, 1)].rearrange("a p c n -> p (a c) n"), x1g[:]).then_inc(x1_kept, 16)

        @block.tensor
        def _(pe):
            def project(dst, w, src):
                for oc in range(KC):
                    for kc in range(KC):
                        mm = pe.matmul(dst[:, oc, :], w[:, kc, oc * P:(oc + 1) * P], src[:, kc, :],
                                       start=(kc == 0), stop=(kc == KC - 1))
                return mm

            def average(dst, src):
                for kc in range(KC):
                    mm = pe.matmul(dst, mean_w[:, :], src[:, kc, :], start=(kc == 0), stop=(kc == KC - 1))
                return mm

            def condition(g, batches):
                if batches[0] == 0:
                    pe.wait_ge(x_loaded, g * 16 + 16)
                    pe.wait_ge(wc_loaded, g * (16 * GB) + 16 * GB)
                for b in batches:
                    for oc in range(KC):
                        for kc in range(KC):
                            mm = pe.matmul(pf[:, oc, b * L:(b + 1) * L], wc[:, b, kc * D + oc * P:kc * D + (oc + 1) * P],
                                           xg[:, kc, b * L:(b + 1) * L], start=(kc == 0), stop=(kc == KC - 1))
                if batches[-1] == GB - 1:
                    mm.then_inc(cond_done, 1)

            def queries(g):
                pe.wait_ge(y_ready, g + 1)
                project(pf, wq, yT).then_inc(q_done, 1)

            def keys(g):
                pe.wait_ge(q_ready, g + 1)
                project(pf, wk, yT).then_inc(k_done, 1)

            def values(g):
                pe.wait_ge(k_ready, g + 1)
                pvw = pf[:].rearrange("p c (b n) -> p (c b) n", n=P)
                for b in range(GB):
                    for kc in range(KC):
                        for u in range(2):
                            mm = pe.matmul(pvw[u * L:(u + 1) * L, b, :], yT[:, kc, b * L:(b + 1) * L], wv[:, kc, u, :],
                                           start=(kc == 0), stop=(kc == KC - 1))
                mm.then_inc(v_done, 1)

            def scores(g, tiles):
                for t in tiles:
                    c = t // TC
                    if t % TC == 0:
                        pe.wait_ge(k_ready, g + 1)
                        pe.wait_ge(qm_loaded[c], g * (16 * HC) + 16 * HC)
                    wait(pe, s_copied, g * NTILE + t)
                    for n in range(TB):
                        b = (t % TC) * TB + n
                        for u in range(2):
                            mm = pe.matmul(ps[u * L:(u + 1) * L, n * PC * L:(n + 1) * PC * L],
                                           kT[:, c, b * L:(b + 1) * L], qm[:, c, b, u, :, :], start=True, stop=True)
                    mm.then_inc(s_done, 1)

            def weighted(g, p):
                m = slice(32 * (p % PC), 32 * (p % PC) + 32)
                pe.wait_ge(w_ready, g * NP + (p + 1))
                if p == 0:
                    pe.wait_ge(v_ready, g + 1)
                if p % PC == 0:
                    wait(pe, att_ready, g * KC + p // PC)
                for b in range(GB):
                    pe.matmul(pnum[m, b * L:(b + 1) * L], vz[:, b, p, :], sc[:, p, b, :], start=True, stop=True)
                pe.matmul(pden[m, :], pair_ones[:, :], sc[:, p, :, :], start=True, stop=True).then_inc(pv_done, 1)

            def output_projection(g):
                pe.wait_ge(att_ready, g * KC + KC)
                project(pr, wo, att).then_inc(o_done, 1)

            def mean(g, n):
                pe.wait_ge((o_ready, x2_ready)[n], g + 1)
                average(pr[:, 0, :], oT).then_inc(mean_done, 1)

            def variance(g, n):
                pe.wait_ge(sq_ready, g * 2 + (n + 1))
                average(pr[:, 1, :], sq).then_inc(var_done, 1)

            def adapter_down(g):
                pe.wait_ge(x1_ready, g + 1)
                pe.wait_ge(wa_loaded, g * (32 * GB) + 32 * GB)
                for b in range(GB):
                    for kc in range(KC):
                        mm = pe.matmul(pr[0:A, 0, b * L:(b + 1) * L], wa[:, b, kc * A:(kc + 1) * A],
                                       x1g[:, kc, b * L:(b + 1) * L], start=(kc == 0), stop=(kc == KC - 1))
                mm.then_inc(down_done, 1)

            def adapter_up(g):
                pe.wait_ge(h_ready, g + 1)
                for b in range(GB):
                    for oc in range(KC):
                        mm = pe.matmul(pr[:, oc, b * L:(b + 1) * L], w2[:, b, oc * P:(oc + 1) * P], hT[:, b, :],
                                       start=True, stop=True)
                mm.then_inc(up_done, 1)

            def input_gates(g, t):
                for kc in range(KC):
                    for u in range(2):
                        pe.matmul(pgate[u * L:(u + 1) * L, :], zT[:, kc, t * L:(t + 1) * L],
                                  gate_w[:, kc, u, :], start=(kc == 0), stop=False)

            def state_gates(g, t):
                wait(pe, ct_ready, g * GB + t)
                for kc in range(KC):
                    for u in range(2):
                        mm = pe.matmul(pgate[u * L:(u + 1) * L, :], cT[:, kc, :], gate_u[:, kc, u, :],
                                       start=False, stop=(kc == KC - 1))
                mm.then_inc(gate_done, 1)

            def state_transposed(g, t):
                pe.wait_ge(c_ready, g * GB + (t + 1))
                pe.transpose(pct, cst[:, :], eye[:, :]).then_inc(ct_done, 1)

            def output_part(g):
                pe.wait_ge(z_ready, g + 1)
                project(pr, wout, zT).then_inc(go_done, 1)

            pe.wait_ge(const_in, CONST_IN)
            pe.wait_ge(setup_pool, 6)
            condition(0, range(GB))
            queries(0)
            keys(0)
            scores(0, range(TC))

            def step(i, rest, attention, front):
                r, a, f = i - 1, i, i + 1
                half = GB // 2
                if rest:
                    weighted(r, NP - 1)
                    output_projection(r)
                if attention:
                    values(a)
                    scores(a, range(TC, NTILE))
                if rest:
                    mean(r, 0)
                if front:
                    pe.wait_ge(v_ready, a + 1)
                    condition(f, range(half))
                if rest:
                    variance(r, 0)
                if front:
                    condition(f, range(half, GB))
                if attention:
                    weighted(a, 0)
                if rest:
                    adapter_down(r)
                if front:
                    queries(f)
                if attention:
                    weighted(a, 1)
                if rest:
                    adapter_up(r)
                if rest:
                    mean(r, 1)
                if front:
                    keys(f)
                if attention:
                    weighted(a, 2)
                if rest:
                    variance(r, 1)
                for s in range(STEP_SLOT, NP):
                    t = 2 * (s - STEP_SLOT)
                    if rest:
                        if t == 0:
                            output_part(r)
                        input_gates(r, t)
                        state_gates(r, t)
                    if attention:
                        weighted(a, s - 1)
                    if rest:
                        if t == 0:
                            pe.wait_ge(go_kept, r + 1)
                        state_transposed(r, t)
                        input_gates(r, t + 1)
                        state_gates(r, t + 1)
                    if front and s in (5, 6):
                        scores(f, range(TC // 2 * (s - 5), TC // 2 * (s - 4)))
                    if rest:
                        state_transposed(r, t + 1)
                if rest:
                    pe.wait_ge(ct_ready, r * GB + GB)

            rounds(pe, step)
            for oc in range(KC):
                for kc in range(KC):
                    mm = pe.matmul(pr[:, oc, 0:L], uout[:, kc, oc * P:(oc + 1) * P], cT[:, kc, :],
                                   start=(kc == 0), stop=(kc == KC - 1))
            mm.then_inc(hoc_done, 1)

        @block.scalar
        def _(act):
            def queries(g):
                act.wait_ge(q_done, g + 1)
                for c in range(KC):
                    op = act.activation(qT[:, c, :], pf[:, c, :], ACT.Identity, scale=qs[:, 0:1], bias=bqs[:, c:c + 1])
                op.then_inc(q_ready, 1)

            def keys(g):
                act.wait_ge(k_done, g + 1)
                for c in range(KC):
                    op = act.activation(kT[:, c, :], pf[:, c, :], ACT.Identity, bias=scal(C_BK + c))
                op.then_inc(k_ready, 1)

            def copy_scores(g, tiles):
                for t in tiles:
                    c, b = t // TC, (t % TC) * TB
                    act.wait_ge(s_done, g * NTILE + (t + 1))
                    act.activation(sc[:, c * PC:(c + 1) * PC, b:b + TB, :].rearrange("p k b n -> p b k n"),
                                   ps[:, :].rearrange("p (b k n) -> p b k n", b=TB, k=PC), ACT.Copy).then_inc(s_copied, 1)

            def sines(g, p):
                act.wait_ge(angle_ready, g * NP + (p + 1))
                a = ang[:, p % 2, :, :].rearrange("p f n -> p (f n)")
                act.activation(a.bitcast(F32), a, ACT.Sin, scale=2 * PI_LOW / TURN, bias=qs[:, 3:4]).then_inc(sine_ready, 1)

            def weights(g, p):
                act.wait_ge(score_ready, g * NP + (p + 1))
                w = sc[:, p, :, :].rearrange("p b n -> p (b n)")
                act.activation(w, w, ACT.Sigmoid).then_inc(w_ready, 1)

            def output_bias(g):
                act.wait_ge(o_done, g + 1)
                for c in range(KC):
                    op = act.activation(oT[:, c, :], pr[:, c, :], ACT.Identity, bias=scal(C_BO + c))
                op.then_inc(o_ready, 1)

            def squares(g, n):
                act.wait_ge(dev_ready, g * 2 + (n + 1))
                act.activation(sq[:], oT[:], ACT.Square).then_inc(sq_ready, 1)

            def deviation(g, n):
                act.wait_ge(var_done, g * 2 + (n + 1))
                act.activation(rstd[:, :], pr[:, 1, :], ACT.Sqrt, bias=scal(C_EPS)).then_inc(std_ready, 1)

            def keep_output_part(g):
                act.wait_ge(go_done, g + 1)
                act.activation(go_all[:, bass.ds(g, 1), :, :].rearrange("p a c n -> p (a c n)"),
                               pr[:].rearrange("p c n -> p (c n)"), ACT.Copy).then_inc(go_kept, 1)

            def gates(g, t):
                act.wait_ge(pre_ready, g * GB + (t + 1))
                act.activation(gat[:, 0:2 * P], pre[:, 0:2 * P], ACT.Sigmoid).then_inc(gate_ready, 1)
                act.activation(gat[:, 2 * P:3 * P], pre[:, 2 * P:3 * P], ACT.Tanh).then_inc(gate_ready, 1)

            act.wait_ge(const_in, CONST_IN)
            act.wait_ge(setup_dve, 1)
            queries(0)
            keys(0)
            copy_scores(0, range(TC))
            sines(0, 0)

            def step(i, rest, attention, front):
                r, a, f = i - 1, i, i + 1
                for s in range(NP):
                    t = 2 * (s - STEP_SLOT)
                    if rest and t == 0:
                        keep_output_part(r)
                    if rest and t >= 0:
                        gates(r, t)
                    if attention and s + 1 < NP:
                        sines(a, s + 1)
                    elif front:
                        sines(f, 0)
                    if rest and s == 0:
                        output_bias(r)
                    if attention and s == 0:
                        copy_scores(a, range(TC, NTILE))
                    if rest and s in (1, 3):
                        squares(r, s // 2)
                        deviation(r, s // 2)
                    if front and s == 2:
                        queries(f)
                    if front and s == 3:
                        keys(f)
                    if rest and t >= 0:
                        gates(r, t + 1)
                    if attention:
                        weights(a, s)
                    if front and s in (5, 6):
                        copy_scores(f, range(TC // 2 * (s - 5), TC // 2 * (s - 4)))

            rounds(act, step)
            act.wait_ge(hoc_done, 1)
            for c in range(KC):
                act.activation(hoc[:, c, :], pr[:, c, 0:L], ACT.Identity, bias=scal(C_BOUT + c)).then_inc(hoc_ready, 1)
            with act.Fori(0, NG) as g:
                act.wait_ge(tail_sum, g * KC + KC)
                go = go_all[:, bass.ds(g, 1), :, :].rearrange("p a c n -> p (a c n)")
                act.activation(go, go, ACT.Tanh).then_inc(tail_tanh, 1)

        @block.vector
        def _(dve):
            done = [0]

            def setup(ins):
                done[0] += 1
                ins.then_inc(setup_link, 1)
                dve.wait_ge(setup_link, done[0])

            dve.wait_ge(const_in, CONST_IN)
            setup(dve.scalar_tensor_tensor(out=qs[:, 1:2], in0=scal(C_TEMP), scalar=-1.0, in1=scal(C_TEMP), op0=ALU.mult,
                                           op1=ALU.max))
            setup(dve.tensor_scalar(qs[:, 1:2], qs[:, 1:2], 0.1, None, ALU.add))
            setup(dve.reciprocal(qs[:, 2:3], qs[:, 1:2]))
            setup(dve.tensor_scalar(qs[:, 0:1], qs[:, 2:3], 1.0 / math.sqrt(HD), None, ALU.mult))
            setup(dve.memset(qs[:, 3:4], -PI_LOW))
            setup(dve.tensor_scalar(bqs[:, :], small[:, C_BQ:C_BQ + KC], qs[:, 0:1], None, ALU.mult))
            phi = small[:, C_PHI:C_PHI + NP * NF]
            setup(dve.tensor_scalar(turns[:, :], phi, 1 / (2 * math.pi), ROUND, ALU.mult, ALU.add))
            setup(dve.tensor_scalar(turns[:, :], turns[:, :], ROUND, None, ALU.subtract))
            setup(dve.scalar_tensor_tensor(out=phase[:, :], in0=turns[:, :], scalar=-TWO_PI_HI, in1=phi,
                                           op0=ALU.mult, op1=ALU.add))
            setup(dve.scalar_tensor_tensor(out=phase[:, :], in0=turns[:, :], scalar=-TWO_PI_LO, in1=phase[:, :],
                                           op0=ALU.mult, op1=ALU.add))
            dve.tensor_scalar(phase[:, :], phase[:, :], TURN / (2 * math.pi), TURN / 2, ALU.mult,
                              ALU.add).then_inc(setup_dve, 1)
            dve.wait_ge(setup_dve, 1)
            dve.wait_ge(setup_pool, 6)

            def conditioned(g):
                dve.wait_ge(cond_done, g + 1)
                for c in range(KC):
                    bias = wc[:, :, KC * D + c:KC * D + c + 1].to_broadcast([P, GB, L])
                    op = dve.tensor_tensor(by_batch(yT[:, c, :]), by_batch(pf[:, c, :]), bias, ALU.add)
                op.then_inc(y_ready, 1)

            def values(g):
                dve.wait_ge(v_done, g + 1)
                vw = pf[:].rearrange("p c (b k d) -> p (c b) k d", k=NP, d=HD)
                for u in range(2):
                    r = slice(u * L, (u + 1) * L)
                    bias = bv[r, :].rearrange("p (o k d) -> p o k d", o=1, d=HD).to_broadcast([L, GB, NP, HD])
                    op = dve.tensor_tensor(vz[r, :, :, u * HD:(u + 1) * HD], vw[r], bias, ALU.add)
                op.then_inc(v_ready, 1)

            def pair(p):
                return sc[:, p, :, :].rearrange("p b n -> p (b n)")

            def angles(g, p):
                if p % PC == 0:
                    dve.wait_ge(s_copied, g * NTILE + TC * (p // PC + 1))
                wait(dve, score_ready, g * NP + (p - 1))
                for f in range(NF):
                    dve.tensor_scalar(ang[:, p % 2, f, :], pair(p), TURN / FREQS[f],
                                      phase[:, p * NF + f:p * NF + f + 1], ALU.mult, ALU.add).then_inc(angle_raw, 1)

            def wrap(g, p):
                dve.wait_ge(angle_raw, g * (NP * NF) + NF * (p + 1))
                a = ang[:, p % 2, :, :].rearrange("p f n -> p (f n)")
                dve.tensor_scalar(a, a, (1 << TURN_BITS) - 1, None, ALU.bitwise_and).then_inc(angle_ready, 1)

            def add_sine(g, p, f):
                amp = scal(C_ALPHA + p * NF + f)
                sine = ang[:, p % 2, f, :].bitcast(F32)
                if f == 0:
                    dve.wait_ge(sine_ready, g * NP + (p + 1))
                    dve.tensor_scalar(pair(p), sine, amp, None, ALU.mult).then_inc(score_part, 1)
                    return
                dve.wait_ge(score_part, g * (NP * (NF - 1)) + (p * (NF - 1) + f))
                op = dve.scalar_tensor_tensor(out=pair(p), in0=sine, scalar=amp, in1=pair(p), op0=ALU.mult, op1=ALU.add)
                op.then_inc(score_ready if f == NF - 1 else score_part, 1)

            def divided(g, c):
                n = g * (2 * KC) + 2 * c
                dve.wait_ge(pv_done, g * NP + PC * (c + 1))
                dve.tensor_scalar(rden[:, :], pden[:, :], EPS_W, None, ALU.add).then_inc(att_part, 1)
                dve.wait_ge(att_part, n + 1)
                dve.reciprocal(rden[:, :], rden[:, :]).then_inc(att_part, 1)
                dve.wait_ge(att_part, n + 2)
                dve.tensor_tensor(att[:, c, :], pnum[:, :], rden[:, :], ALU.mult).then_inc(att_ready, 1)
                dve.wait_ge(att_ready, g * KC + (c + 1))

            links = [0]

            def link(g, ins):
                links[0] += 1
                ins.then_inc(rest_link, 1)
                dve.wait_ge(rest_link, g * LINKS + links[0])

            def less_mean(g, n):
                dve.wait_ge(mean_done, g * 2 + (n + 1))
                for c in range(KC):
                    op = dve.tensor_tensor(oT[:, c, :], oT[:, c, :], pr[:, 0, :], ALU.subtract)
                op.then_inc(dev_ready, 1)

            def reciprocal_deviation(g, n):
                dve.wait_ge(dev_ready, g * 2 + (n + 1))
                dve.wait_ge(std_ready, g * 2 + (n + 1))
                link(g, dve.reciprocal(rstd[:, :], rstd[:, :]))

            def residual(g):
                reciprocal_deviation(g, 0)
                dve.wait_ge(xr_loaded, g * 16 + 16)
                for c in range(KC):
                    link(g, dve.scalar_tensor_tensor(out=oT[:, c, :], in0=oT[:, c, :], scalar=scal(C_GAMMA + c),
                                                     in1=rstd[:, :], op0=ALU.mult, op1=ALU.mult))
                for c in range(KC):
                    op = dve.scalar_tensor_tensor(out=x1g[:, c, :], in0=oT[:, c, :], scalar=scal(C_BETA + c),
                                                  in1=xr[:, c, :], op0=ALU.add, op1=ALU.add)
                op.then_inc(x1_ready, 1)

            def hidden(g):
                dve.wait_ge(down_done, g + 1)
                link(g, dve.tensor_tensor(hT[:], by_batch(pr[0:A, 0, :]), w2[:, :, D:D + 1].to_broadcast([A, GB, L]), ALU.add))
                dve.tensor_scalar(hT[:], hT[:], 0.0, None, ALU.max).then_inc(h_ready, 1)

            def of_language(c, k):
                col = KC * A + KC * k + c
                return wa[:, :, col:col + 1].to_broadcast([P, GB, L])

            def adapted(g):
                dve.wait_ge(up_done, g + 1)
                dve.wait_ge(x1_ready, g + 1)
                for c in range(KC):
                    link(g, dve.tensor_tensor(oT[:, c, :], x1g[:, c, :], pr[:, c, :], ALU.add))
                for c in range(KC):
                    op = dve.tensor_tensor(by_batch(oT[:, c, :]), by_batch(oT[:, c, :]), of_language(c, 0), ALU.add)
                op.then_inc(x2_ready, 1)
                dve.wait_ge(x2_ready, g + 1)

            def modulated(g):
                reciprocal_deviation(g, 1)
                for c in range(KC):
                    link(g, dve.tensor_tensor(oT[:, c, :], oT[:, c, :], rstd[:, :], ALU.mult))
                for c in range(KC):
                    link(g, dve.tensor_tensor(by_batch(oT[:, c, :]), by_batch(oT[:, c, :]), of_language(c, 1), ALU.mult))
                for c in range(KC):
                    op = dve.tensor_tensor(by_batch(zT[:, c, :]), by_batch(oT[:, c, :]), of_language(c, 2), ALU.add)
                op.then_inc(z_ready, 1)
                dve.wait_ge(z_ready, g + 1)
                dve.wait_ge(x1_kept, g * 16 + 16)
                dve.sem_inc(rest_free, 1)

            def gate_sum(g, t):
                dve.wait_ge(gate_done, g * GB + (t + 1))
                dve.tensor_tensor(pre[:, :], pgate, gate_b[:, :], ALU.add).then_inc(pre_ready, 1)

            def cell_step(g, t):
                dve.wait_ge(gate_ready, g * (2 * GB) + (2 * t + 1))
                dve.tensor_tensor(fc[:, 0, :], gat[:, 0:P], cst[:, :], ALU.mult).then_inc(cell, 1)
                dve.wait_ge(gate_ready, g * (2 * GB) + (2 * t + 2))
                dve.tensor_tensor(fc[:, 1, :], gat[:, P:2 * P], gat[:, 2 * P:3 * P], ALU.mult).then_inc(cell, 1)
                dve.wait_ge(cell, g * (2 * GB) + (2 * t + 2))
                dve.tensor_tensor(cst[:, :], fc[:, 0, :], fc[:, 1, :], ALU.add).then_inc(c_ready, 1)

            def state_copy(g, t):
                dve.wait_ge(ct_done, g * GB + (t + 1))
                dve.tensor_copy(cT[:].rearrange("p c n -> p (c n)"), pct).then_inc(ct_ready, 1)

            conditioned(0)
            angles(0, 0)
            wrap(0, 0)

            def step(i, rest, attention, front):
                r, a, f = i - 1, i, i + 1
                links[0] = 0
                for s in range(NP):
                    t = 2 * (s - STEP_SLOT)
                    steps = rest and t >= 0
                    if attention and s + 1 < NP:
                        angles(a, s + 1)
                    elif front:
                        angles(f, 0)
                    if rest and s == 0:
                        divided(r, KC - 1)
                    if rest and s == 1:
                        less_mean(r, 0)
                    if rest and s == 2:
                        hidden(r)
                    if rest and s == 3:
                        less_mean(r, 1)
                    if steps:
                        gate_sum(r, t)
                    if attention and s + 1 < NP:
                        wrap(a, s + 1)
                    elif front:
                        wrap(f, 0)
                    if attention and s == 0:
                        values(a)
                    if front and s == 2:
                        conditioned(f)
                    if attention and s == PC + 1:
                        divided(a, 0)
                    if steps:
                        cell_step(r, t)
                    if attention:
                        add_sine(a, s, 0)
                        add_sine(a, s, 1)
                    if steps:
                        state_copy(r, t)
                    if attention:
                        add_sine(a, s, 2)
                        add_sine(a, s, 3)
                    if rest and s == 1:
                        residual(r)
                    if rest and s == 2:
                        adapted(r)
                    if rest and s == 3:
                        modulated(r)
                    if steps:
                        gate_sum(r, t + 1)
                    if attention:
                        add_sine(a, s, 4)
                    if steps:
                        cell_step(r, t + 1)
                        state_copy(r, t + 1)
                assert not rest or links[0] == LINKS, links[0]

            rounds(dve, step)
            dve.wait_ge(hoc_ready, KC)
            dve.wait_ge(x1_loaded, 16)
            with dve.Fori(0, NG) as g:
                for c in range(KC):
                    go = go_all[:, bass.ds(g, 1), c, :].rearrange("p a (t n) -> p (a t) n", n=L)
                    dve.tensor_tensor(go, go, hoc[:, c:c + 1, :].to_broadcast([P, GB, L]), ALU.add).then_inc(tail_sum, 1)
                dve.wait_ge(tail_tanh, g + 1)
                go = go_all[:, bass.ds(g, 1), :, :].rearrange("p a c n -> p (a c n)")
                x1 = x1_all[:, bass.ds(g, 1), :].rearrange("p a n -> p (a n)")
                dve.tensor_tensor(go, go, x1, ALU.add).then_inc(tail_out, 1)


_OUT = (NG, P, KC, NT)


def kernel(**inputs):
    import numpy as np
    import concourse.bacc as bacc
    from concourse.bass_utils import run_bass_kernel_spmd

    a = {k: np.asarray(v) for k, v in inputs.items()}

    def chunked(w):
        o, i = w.shape
        return w.T.reshape(i // P, P, o).transpose(1, 0, 2)

    def cols(v):
        return v.reshape(KC, P).T

    x = a["x"].reshape(NG, NT, KC, P).transpose(0, 3, 2, 1)
    ids = np.concatenate([a["itok_B_0_7"], a["itok_B_0_8"]]).reshape(1, 2 * B)
    rows = np.concatenate([a["L0_attn_temperature"], np.full(1, EPS_LN, np.float32)])

    def by_pair(v):
        v = v.reshape(NP, 2, NF).transpose(1, 0, 2).reshape(2, 1, NP * NF)
        return np.broadcast_to(v, (2, L, NP * NF)).reshape(P, NP * NF)

    small = np.concatenate([cols(a["L0_attn_bq"]), cols(a["L0_attn_bk"]), cols(a["L0_attn_bo"]), cols(a["L0_attn_gamma"]),
                            cols(a["L0_attn_beta"]), cols(a["L0_ffn_bo"]), np.broadcast_to(rows, (P, rows.size)),
                            by_pair(a["L0_attn_alpha"]), by_pair(a["L0_attn_phi"])], axis=1)
    cond = a["L0_cond_weight"].transpose(0, 2, 1).reshape(NSUB, KC, P, D).transpose(0, 2, 1, 3).reshape(NSUB, P, KC * D)
    cond = np.concatenate([cond, a["L0_cond_bias"].reshape(NSUB, KC, P).transpose(0, 2, 1)], axis=2)
    down = a["L0_cond2_W1"].reshape(NLANG, KC, P, A).transpose(0, 2, 1, 3).reshape(NLANG, P, KC * A)
    down = np.concatenate([down] + [a["L0_cond2_" + n].reshape(NLANG, KC, P).transpose(0, 2, 1) for n in ("b2", "gamma", "beta")], axis=2)
    up = np.concatenate([a["L0_cond2_W2"], a["L0_cond2_b1"][:, :, None]], axis=2)
    wv = chunked(a["L0_attn_Wv"]).reshape(P, KC, NP, 2, HD).transpose(0, 1, 3, 2, 4).reshape(P, KC, 2, P)
    bv = a["L0_attn_bv"].reshape(NP, 2, HD).transpose(1, 0, 2).reshape(2, 1, P)

    def gate_cols(ws):
        w = np.stack([chunked(w).reshape(P, KC, 2, P) for w in ws], axis=3)
        return w.reshape(P, KC, 2, GATES * P)

    gate_b = np.stack([a["L0_ffn_" + n].reshape(2, P) for n in ("bf", "bi", "bc")], axis=1).reshape(2, 1, GATES * P)
    arrays = {
        "x": x, "ids": ids, "small": small, "cond": cond, "down": down, "up": up,
        "wq": chunked(a["L0_attn_Wq"]), "wk": chunked(a["L0_attn_Wk"]), "wv": wv,
        "bv": np.broadcast_to(bv, (2, L, P)).reshape(P, P), "wo": chunked(a["L0_attn_Wo"]),
        "gate_w": gate_cols([a["L0_ffn_" + n] for n in ("wf", "wi", "wc")]),
        "gate_u": gate_cols([a["L0_ffn_" + n] for n in ("uf", "ui", "uc")]),
        "gate_b": np.broadcast_to(gate_b, (2, L, GATES * P)).reshape(P, GATES * P),
        "c0": np.broadcast_to(a["L0_ffn_in_c"].reshape(2, 1, P), (2, L, P)).reshape(P, P),
        "c0t": np.broadcast_to(cols(a["L0_ffn_in_c"])[:, :, None], (P, KC, L)),
        "wout": chunked(a["L0_ffn_wo"]), "uout": chunked(a["L0_ffn_uo"]), "eye": np.eye(P, dtype=np.float32),
    }
    nc = bacc.Bacc("TRN2", target_bir_lowering=False, num_devices=1)
    feeds, args = {}, []
    for name, v in arrays.items():
        v = np.ascontiguousarray(v)
        feeds[f"in_{name}"] = v
        args.append(nc.dram_tensor(f"in_{name}", v.shape, mybir.dt.from_np(v.dtype), kind="ExternalInput").ap())
    args.append(nc.dram_tensor("out_t", _OUT, F32, kind="ExternalOutput").ap())
    build(nc, *args)
    r = run_bass_kernel_spmd(nc, [feeds], core_ids=[0])
    got = r.results[0]["out_t"]
    return got.transpose(0, 3, 2, 1).reshape(B, L, D)
```

```python
import math
from contextlib import ExitStack

import concourse.bass as bass
from concourse import mybir

P = 128
F32 = mybir.dt.float32
I32 = mybir.dt.int32
ALU = mybir.AluOpType
ACT = mybir.ActivationFunctionType

B, L, D = 32, 64, 256
KC = D // P
H, HD = 16, 16
GB = 8
NG = B // GB
NT = GB * L
HC = H // KC
NP = H // 2
PC = NP // KC
TB = 2
TC = GB // TB
NTILE = KC * TC
A = 64
NF = 5
FREQS = (31.0, 37.0, 41.0, 43.0, 47.0)
NSUB, NLANG = 8, 10
EPS_LN, EPS_W = 1e-5, 1e-10
GATES = 3
WC_COLS = KC * D + KC
WA_COLS = KC * A + 3 * KC
W2_COLS = D + 1

TURN_BITS = 20
TURN = float(1 << TURN_BITS)
PI_LOW = 3.1415925
ROUND = 1.5 * 2.0 ** 23
TWO_PI_HI = 6.28125
TWO_PI_LO = 2 * math.pi - TWO_PI_HI

C_BQ, C_BK, C_BO, C_GAMMA, C_BETA, C_BOUT = 0, 2, 4, 6, 8, 10
C_TEMP, C_EPS = 12, 13
C_ALPHA = 14
C_PHI = C_ALPHA + NP * NF
C_COLS = C_PHI + NP * NF

LINKS = 11
REC_SLOT = 5
UNITS = 2 * NF + 1
WEIGHTED_AT = {1: 4, 4: 5, 7: 6}
TILE_AT = {1: 0, 2: 1, 3: 2, 4: 3}
SINES_AT = {1: 6, 4: 7, 6: 8}
WEIGHTS_AT = {2: 5, 5: 6, 7: 7}


def wait(eng, sem, value):
    if not (isinstance(value, int) and value <= 0):
        eng.wait_ge(sem, value)


def build(nc, x_in, ids_in, small_in, cond_in, down_in, up_in, wq_in, wk_in, wv_in, bv_in, wo_in,
          gate_w_in, gate_u_in, gate_b_in, c0_in, c0t_in, wout_in, uout_in, eye_in, out):
    with ExitStack() as ctx:
        def sb(name, shape, dt=F32):
            return ctx.enter_context(nc.sbuf_tensor(name, shape, dt))

        def pb(name, shape, dt=F32):
            return ctx.enter_context(nc.psum_tensor(name, shape, dt))

        def sem(name):
            return ctx.enter_context(nc.semaphore(name))

        ids = sb("ids", [1, 2 * B], I32)
        small = sb("small", [P, C_COLS])
        wq = sb("wq", [P, KC, D])
        wk = sb("wk", [P, KC, D])
        wv = sb("wv", [P, KC, 2, P])
        bv = sb("bv", [P, P])
        wo = sb("wo", [P, KC, D])
        gate_w = sb("gate_w", [P, KC, 2, GATES * P])
        gate_u = sb("gate_u", [P, KC, 2, GATES * P])
        gate_b = sb("gate_b", [P, GATES * P])
        wout = sb("wout", [P, KC, D])
        uout = sb("uout", [P, KC, D])
        eye = sb("eye", [P, P])
        mean_w = sb("mean_w", [P, P])
        pair_ones = sb("pair_ones", [P, 32])
        qs = sb("qs", [P, 4])
        bqs = sb("bqs", [P, KC])
        phase = sb("phase", [P, NP * NF])
        turns = sb("turns", [P, NP * NF])
        xg = sb("xg", [P, KC, NT])
        wc = sb("wc", [P, GB, WC_COLS])
        yT = sb("yT", [P, KC, NT])
        qT = sb("qT", [P, KC, NT])
        kT = sb("kT", [P, KC, NT])
        qm = sb("qm", [P, KC, GB, 2, PC, L])
        vz = sb("vz", [P, GB, NP, 32])
        sc = sb("sc", [P, NP, GB, L])
        ang = sb("ang", [P, 2, NF, NT], I32)
        att = sb("att", [P, KC, NT])
        rden = sb("rden", [P, NT])
        xr = sb("xr", [P, KC, NT])
        wa = sb("wa", [P, GB, WA_COLS])
        w2 = sb("w2", [A, GB, W2_COLS])
        oT = sb("oT", [P, KC, NT])
        sq = sb("sq", [P, KC, NT])
        rstd = sb("rstd", [P, NT])
        x1g = sb("x1g", [P, KC, NT])
        hT = sb("hT", [A, GB, L])
        zT = sb("zT", [P, KC, NT])
        x1_dram = nc.dram_tensor("x1_kept", (NG, P, KC, NT), F32, kind="Internal").ap()
        x1_all = qm[:].rearrange("p c b u k n -> p (c b u k n)").rearrange("p (o g n) -> p o g n", o=2, g=NG)[:, 0]
        go_all = sb("go_all", [P, NG, KC, NT])
        cst = sb("cst", [P, P])
        cT = sb("cT", [P, KC, L])
        pre = sb("pre", [P, GATES * P])
        gat = sb("gat", [P, GATES * P])
        fc = sb("fc", [P, 2, P])
        hoc = sb("hoc", [P, KC, L])

        pf = pb("pf", [P, KC, NT])
        pr = pb("pr", [P, KC, NT])
        ps = pb("ps", [P, NT])
        pnum = pb("pnum", [P, NT])
        pden = pb("pden", [P, NT])
        pgate = pb("pgate", [P, NT])
        pgates = (pgate[:, 0:GATES * P], pr[:, 0, 0:GATES * P])
        pct = pr[:, 1, 0:P]

        small_in_s, front_in, attention_in, rest_in = sem("small_in"), sem("front_in"), sem("attention_in"), sem("rest_in")
        ids_s, setup_pool, setup_dve = sem("ids_loaded"), sem("setup_pool"), sem("setup_dve")
        setup_link, rest_link = sem("setup_link"), sem("rest_link")
        x_loaded, wc_loaded, xr_loaded, wa_loaded = sem("x_loaded"), sem("wc_loaded"), sem("xr_loaded"), sem("wa_loaded")
        rest_free = sem("rest_free")
        cond_done, y_ready, q_done, q_ready = sem("cond_done"), sem("y_ready"), sem("q_done"), sem("q_ready")
        qm_loaded = [sem(f"qm_loaded{c}") for c in range(KC)]
        k_done, k_ready, v_done, v_ready = sem("k_done"), sem("k_ready"), sem("v_done"), sem("v_ready")
        s_done, s_copied = sem("s_done"), sem("s_copied")
        angle_raw, angle_ready, sine_ready = sem("angle_raw"), sem("angle_ready"), sem("sine_ready")
        score_part, score_ready, w_ready = sem("score_part"), sem("score_ready"), sem("w_ready")
        pv_done, att_part, att_ready = sem("pv_done"), sem("att_part"), sem("att_ready")
        o_done, o_ready = sem("o_done"), sem("o_ready")
        mean_done, dev_ready, sq_ready = sem("mean_done"), sem("dev_ready"), sem("sq_ready")
        var_done, std_ready = sem("var_done"), sem("std_ready")
        x1_ready, x1_kept, down_done, h_ready = sem("x1_ready"), sem("x1_kept"), sem("down_done"), sem("h_ready")
        up_done, x2_ready, z_ready = sem("up_done"), sem("x2_ready"), sem("z_ready")
        go_done, go_kept = sem("go_done"), sem("go_kept")
        gate_done, pre_ready, gate_ready, cell = sem("gate_done"), sem("pre_ready"), sem("gate_ready"), sem("cell")
        c_ready, ct_done, ct_ready = sem("c_ready"), sem("ct_done"), sem("ct_ready")
        x1_loaded = sem("x1_loaded")
        hoc_done, hoc_ready = sem("hoc_done"), sem("hoc_ready")
        tail_sum, tail_tanh, tail_out, stored = sem("tail_sum"), sem("tail_tanh"), sem("tail_out"), sem("stored")

        front_consts = ((wq, wq_in), (wk, wk_in))
        attention_consts = ((wv, wv_in), (bv, bv_in), (wo, wo_in), (eye, eye_in))
        rest_consts = ((wout, wout_in), (gate_w, gate_w_in), (gate_u, gate_u_in), (gate_b, gate_b_in), (cst, c0_in),
                       (cT, c0t_in), (uout, uout_in))
        block = ctx.enter_context(nc.Block())

        def scal(col):
            return small[:, col:col + 1]

        def by_batch(ap):
            return ap.rearrange("p (b n) -> p b n", b=GB)

        def rounds(eng, step, first=True):
            if first:
                step(0, rest=False, attention=True, front=True)
            with eng.Fori(1, NG - 1) as i:
                step(i, rest=True, attention=True, front=True)
            step(NG - 1, rest=True, attention=True, front=False)
            step(NG, rest=True, attention=False, front=False)

        @block.sync
        def _(sp):
            def load_front(g):
                sp.dma_start(xg[:], x_in[bass.ds(g, 1)].rearrange("a p c n -> p (a c) n")).then_inc(x_loaded, 16)
                for b in range(GB):
                    s = sp.value_load(ids[0:1, bass.ds(g * GB + b, 1)], min_val=0, max_val=NSUB - 1)
                    sp.dma_start(wc[:, b, :], cond_in[bass.ds(s, 1)].rearrange("a p n -> p (a n)")).then_inc(wc_loaded, 16)

            def load_rest(g):
                sp.dma_start(xr[:], x_in[bass.ds(g, 1)].rearrange("a p c n -> p (a c) n")).then_inc(xr_loaded, 16)
                for b in range(GB):
                    s = sp.value_load(ids[0:1, bass.ds(g * GB + (B + b), 1)], min_val=0, max_val=NLANG - 1)
                    sp.dma_start(wa[:, b, :], down_in[bass.ds(s, 1)].rearrange("a p n -> p (a n)")).then_inc(wa_loaded, 16)
                    sp.dma_start(w2[:, b, :], up_in[bass.ds(s, 1)].rearrange("a p n -> p (a n)")).then_inc(wa_loaded, 16)

            def spread_q(g):
                sp.wait_ge(q_ready, g + 1)
                for c in range(KC):
                    for h in range(HC):
                        r = slice(HD * h, HD * h + HD)
                        sp.dma_start(qm[r, c, :, h % 2, h // 2, :], by_batch(qT[r, c, :])).then_inc(qm_loaded[c], 16)

            sp.dma_start(ids[:, :], ids_in).then_inc(ids_s, 16)
            sp.dma_start(small[:], small_in).then_inc(small_in_s, 16)
            sp.wait_ge(ids_s, 16)
            load_front(0)
            for consts, loaded in ((front_consts, front_in), (attention_consts, attention_in), (rest_consts, rest_in)):
                for dst, src in consts:
                    sp.dma_start(dst[:], src).then_inc(loaded, 16)
            sp.wait_ge(setup_pool, 6)
            spread_q(0)

            def step(i, rest, attention, front):
                if front:
                    sp.wait_ge(y_ready, i + 1)
                    load_front(i + 1)
                if rest:
                    sp.wait_ge(rest_free, i)
                    load_rest(i - 1)
                if front:
                    spread_q(i + 1)

            rounds(sp, step)
            sp.wait_ge(s_done, NG * NTILE)
            sp.wait_ge(x1_kept, 16 * NG)
            sp.dma_start(x1_all.rearrange("p g (c n) -> p g c n", c=KC), x1_dram.rearrange("g p c n -> p g c n")).then_inc(x1_loaded, 16)
            with sp.Fori(0, NG) as g:
                sp.wait_ge(tail_out, g + 1)
                sp.dma_start(out[bass.ds(g, 1)].rearrange("a p c n -> p (a c) n"),
                             go_all[:, bass.ds(g, 1), :, :].rearrange("p a c n -> p (a c) n")).then_inc(stored, 16)
            sp.wait_ge(stored, 16 * NG)

        @block.gpsimd
        def _(pool):
            pool.memset(qm[:], 0.0).then_inc(setup_pool, 1)
            pool.memset(mean_w[:], 1.0 / D).then_inc(setup_pool, 1)
            pool.memset(pair_ones[:], 0.0).then_inc(setup_pool, 1)
            pool.memset(vz[:], 0.0).then_inc(setup_pool, 1)
            pool.wait_ge(setup_pool, 4)
            pool.memset(pair_ones[0:L, 0:HD], 1.0).then_inc(setup_pool, 1)
            pool.memset(pair_ones[L:P, HD:2 * HD], 1.0).then_inc(setup_pool, 1)
            pool.wait_ge(setup_pool, 6)
            pool.sem_inc(rest_free, 1)
            with pool.Fori(0, NG) as g:
                pool.wait_ge(x1_ready, g + 1)
                pool.dma_start(x1_dram[bass.ds(g, 1)].rearrange("a p c n -> p (a c) n"), x1g[:]).then_inc(x1_kept, 16)

        @block.tensor
        def _(pe):
            def project(dst, w, src):
                for oc in range(KC):
                    for kc in range(KC):
                        mm = pe.matmul(dst[:, oc, :], w[:, kc, oc * P:(oc + 1) * P], src[:, kc, :],
                                       start=(kc == 0), stop=(kc == KC - 1))
                return mm

            def average(dst, src):
                for kc in range(KC):
                    mm = pe.matmul(dst, mean_w[:, :], src[:, kc, :], start=(kc == 0), stop=(kc == KC - 1))
                return mm

            def condition(g, batches):
                if batches[0] == 0:
                    pe.wait_ge(x_loaded, g * 16 + 16)
                    pe.wait_ge(wc_loaded, g * (16 * GB) + 16 * GB)
                for b in batches:
                    for oc in range(KC):
                        for kc in range(KC):
                            mm = pe.matmul(pf[:, oc, b * L:(b + 1) * L], wc[:, b, kc * D + oc * P:kc * D + (oc + 1) * P],
                                           xg[:, kc, b * L:(b + 1) * L], start=(kc == 0), stop=(kc == KC - 1))
                if batches[-1] == GB - 1:
                    mm.then_inc(cond_done, 1)

            def queries(g):
                pe.wait_ge(y_ready, g + 1)
                project(pf, wq, yT).then_inc(q_done, 1)

            def keys(g):
                pe.wait_ge(q_ready, g + 1)
                project(pf, wk, yT).then_inc(k_done, 1)

            def values(g):
                pe.wait_ge(k_ready, g + 1)
                pvw = pf[:].rearrange("p c (b n) -> p (c b) n", n=P)
                for b in range(GB):
                    for kc in range(KC):
                        for u in range(2):
                            mm = pe.matmul(pvw[u * L:(u + 1) * L, b, :], yT[:, kc, b * L:(b + 1) * L], wv[:, kc, u, :],
                                           start=(kc == 0), stop=(kc == KC - 1))
                mm.then_inc(v_done, 1)

            def scores(g, tiles):
                for t in tiles:
                    c = t // TC
                    if t % TC == 0:
                        pe.wait_ge(k_ready, g + 1)
                        pe.wait_ge(qm_loaded[c], g * (16 * HC) + 16 * HC)
                    wait(pe, s_copied, g * NTILE + t)
                    for n in range(TB):
                        b = (t % TC) * TB + n
                        for u in range(2):
                            mm = pe.matmul(ps[u * L:(u + 1) * L, n * PC * L:(n + 1) * PC * L],
                                           kT[:, c, b * L:(b + 1) * L], qm[:, c, b, u, :, :], start=True, stop=True)
                    mm.then_inc(s_done, 1)

            def weighted(g, p):
                m = slice(32 * (p % PC), 32 * (p % PC) + 32)
                pe.wait_ge(w_ready, g * NP + (p + 1))
                if p == 0:
                    pe.wait_ge(v_ready, g + 1)
                if p % PC == 0:
                    wait(pe, att_ready, g * KC + p // PC)
                for b in range(GB):
                    pe.matmul(pnum[m, b * L:(b + 1) * L], vz[:, b, p, :], sc[:, p, b, :], start=True, stop=True)
                pe.matmul(pden[m, :], pair_ones[:, :], sc[:, p, :, :], start=True, stop=True).then_inc(pv_done, 1)

            def output_projection(g):
                pe.wait_ge(att_ready, g * KC + KC)
                project(pr, wo, att).then_inc(o_done, 1)

            def mean(g, n):
                pe.wait_ge((o_ready, x2_ready)[n], g + 1)
                average(pr[:, 0, :], oT).then_inc(mean_done, 1)

            def variance(g, n):
                pe.wait_ge(sq_ready, g * 2 + (n + 1))
                average(pr[:, 1, :], sq).then_inc(var_done, 1)

            def adapter_down(g):
                pe.wait_ge(x1_ready, g + 1)
                pe.wait_ge(wa_loaded, g * (32 * GB) + 32 * GB)
                for b in range(GB):
                    for kc in range(KC):
                        mm = pe.matmul(pr[0:A, 0, b * L:(b + 1) * L], wa[:, b, kc * A:(kc + 1) * A],
                                       x1g[:, kc, b * L:(b + 1) * L], start=(kc == 0), stop=(kc == KC - 1))
                mm.then_inc(down_done, 1)

            def adapter_up(g):
                pe.wait_ge(h_ready, g + 1)
                for b in range(GB):
                    for oc in range(KC):
                        mm = pe.matmul(pr[:, oc, b * L:(b + 1) * L], w2[:, b, oc * P:(oc + 1) * P], hT[:, b, :],
                                       start=True, stop=True)
                mm.then_inc(up_done, 1)

            def input_gates(g, t):
                for kc in range(KC):
                    for u in range(2):
                        pe.matmul(pgates[t % 2][u * L:(u + 1) * L, :], zT[:, kc, t * L:(t + 1) * L],
                                  gate_w[:, kc, u, :], start=(kc == 0), stop=False)

            def state_gates(g, t):
                wait(pe, ct_ready, g * GB + t)
                for kc in range(KC):
                    for u in range(2):
                        mm = pe.matmul(pgates[t % 2][u * L:(u + 1) * L, :], cT[:, kc, :], gate_u[:, kc, u, :],
                                       start=False, stop=(kc == KC - 1))
                mm.then_inc(gate_done, 1)

            def state_transposed(g, t):
                pe.wait_ge(c_ready, g * GB + (t + 1))
                pe.transpose(pct, cst[:, :], eye[:, :]).then_inc(ct_done, 1)

            def output_part(g):
                project(pf, wout, zT).then_inc(go_done, 1)

            condition(0, range(GB))
            pe.wait_ge(front_in, 16 * len(front_consts))
            queries(0)
            keys(0)
            scores(0, range(TC))
            pe.wait_ge(attention_in, 16 * len(attention_consts))
            pe.wait_ge(setup_pool, 6)

            def step(i, rest, attention, front):
                r, a, f = i - 1, i, i + 1
                half = GB // 2
                if rest:
                    pe.wait_ge(rest_in, 16 * len(rest_consts))
                if rest:
                    weighted(r, NP - 1)
                if attention:
                    values(a)
                    scores(a, range(TC, TC + TC // 2))
                if rest:
                    output_projection(r)
                if attention:
                    scores(a, range(TC + TC // 2, NTILE))
                if rest:
                    mean(r, 0)
                if front:
                    pe.wait_ge(v_ready, a + 1)
                    condition(f, range(half))
                if rest:
                    variance(r, 0)
                if front:
                    condition(f, range(half, GB))
                if attention:
                    weighted(a, 0)
                if front:
                    queries(f)
                if rest:
                    adapter_down(r)
                if attention:
                    weighted(a, 1)
                if rest:
                    adapter_up(r)
                if front:
                    keys(f)
                if rest:
                    mean(r, 1)
                if attention:
                    weighted(a, 2)
                if rest:
                    variance(r, 1)
                if attention:
                    weighted(a, 3)
                if rest:
                    pe.wait_ge(z_ready, r + 1)
                    input_gates(r, 0)
                for t in range(GB):
                    if rest:
                        state_gates(r, t)
                        if t + 1 < GB:
                            input_gates(r, t + 1)
                        if t == 0:
                            output_part(r)
                    if attention and t in WEIGHTED_AT:
                        weighted(a, WEIGHTED_AT[t])
                    if front and t in TILE_AT:
                        scores(f, [TILE_AT[t]])
                    if rest:
                        state_transposed(r, t)
                if rest:
                    pe.wait_ge(ct_ready, r * GB + GB)
                    pe.wait_ge(go_kept, r + 1)

            rounds(pe, step)
            for oc in range(KC):
                for kc in range(KC):
                    mm = pe.matmul(pr[:, oc, 0:L], uout[:, kc, oc * P:(oc + 1) * P], cT[:, kc, :],
                                   start=(kc == 0), stop=(kc == KC - 1))
            mm.then_inc(hoc_done, 1)

        @block.scalar
        def _(act):
            def queries(g):
                act.wait_ge(q_done, g + 1)
                for c in range(KC):
                    op = act.activation(qT[:, c, :], pf[:, c, :], ACT.Identity, scale=qs[:, 0:1], bias=bqs[:, c:c + 1])
                op.then_inc(q_ready, 1)

            def keys(g):
                act.wait_ge(k_done, g + 1)
                for c in range(KC):
                    op = act.activation(kT[:, c, :], pf[:, c, :], ACT.Identity, bias=scal(C_BK + c))
                op.then_inc(k_ready, 1)

            def copy_scores(g, tiles):
                for t in tiles:
                    c, b = t // TC, (t % TC) * TB
                    act.wait_ge(s_done, g * NTILE + (t + 1))
                    act.activation(sc[:, c * PC:(c + 1) * PC, b:b + TB, :].rearrange("p k b n -> p b k n"),
                                   ps[:, :].rearrange("p (b k n) -> p b k n", b=TB, k=PC), ACT.Copy).then_inc(s_copied, 1)

            def sines(g, p):
                act.wait_ge(angle_ready, g * NP + (p + 1))
                a = ang[:, p % 2, :, :].rearrange("p f n -> p (f n)")
                act.activation(a.bitcast(F32), a, ACT.Sin, scale=2 * PI_LOW / TURN, bias=qs[:, 3:4]).then_inc(sine_ready, 1)

            def weights(g, p):
                act.wait_ge(score_ready, g * NP + (p + 1))
                w = sc[:, p, :, :].rearrange("p b n -> p (b n)")
                act.activation(w, w, ACT.Sigmoid).then_inc(w_ready, 1)

            def output_bias(g):
                act.wait_ge(o_done, g + 1)
                for c in range(KC):
                    op = act.activation(oT[:, c, :], pr[:, c, :], ACT.Identity, bias=scal(C_BO + c))
                op.then_inc(o_ready, 1)

            def squares(g, n):
                act.wait_ge(dev_ready, g * 2 + (n + 1))
                act.activation(sq[:], oT[:], ACT.Square).then_inc(sq_ready, 1)

            def deviation(g, n):
                act.wait_ge(var_done, g * 2 + (n + 1))
                act.activation(rstd[:, :], pr[:, 1, :], ACT.Sqrt, bias=scal(C_EPS)).then_inc(std_ready, 1)

            def keep_output_part(g):
                act.wait_ge(go_done, g + 1)
                act.activation(go_all[:, bass.ds(g, 1), :, :].rearrange("p a c n -> p (a c n)"),
                               pf[:].rearrange("p c n -> p (c n)"), ACT.Copy).then_inc(go_kept, 1)

            def gates(g, t):
                act.wait_ge(pre_ready, g * GB + (t + 1))
                act.activation(gat[:, 0:2 * P], pre[:, 0:2 * P], ACT.Sigmoid).then_inc(gate_ready, 1)
                act.activation(gat[:, 2 * P:3 * P], pre[:, 2 * P:3 * P], ACT.Tanh).then_inc(gate_ready, 1)

            act.wait_ge(small_in_s, 16)
            act.wait_ge(setup_dve, 1)
            queries(0)
            keys(0)
            copy_scores(0, range(TC))
            sines(0, 0)

            def step(i, rest, attention, front):
                r, a, f = i - 1, i, i + 1
                for s in range(REC_SLOT):
                    if rest and s == 4:
                        deviation(r, 1)
                    if attention:
                        sines(a, s + 1)
                    if attention and s == 0:
                        copy_scores(a, range(TC, TC + TC // 2))
                    if rest and s == 0:
                        output_bias(r)
                    if attention and s == 0:
                        copy_scores(a, range(TC + TC // 2, NTILE))
                    if rest and s == 1:
                        squares(r, 0)
                        deviation(r, 0)
                    if front and s == 2:
                        queries(f)
                    if front and s == 3:
                        keys(f)
                    if rest and s == 3:
                        squares(r, 1)
                    if attention:
                        weights(a, s)
                for t in range(GB):
                    if rest:
                        gates(r, t)
                        if t == 0:
                            keep_output_part(r)
                    if front and t in TILE_AT:
                        copy_scores(f, [TILE_AT[t]])
                    s = SINES_AT.get(t)
                    if s is not None and attention and s < NP:
                        sines(a, s)
                    if s == NP and front:
                        sines(f, 0)
                    if attention and t in WEIGHTS_AT:
                        weights(a, WEIGHTS_AT[t])

            rounds(act, step)
            act.wait_ge(hoc_done, 1)
            for c in range(KC):
                act.activation(hoc[:, c, :], pr[:, c, 0:L], ACT.Identity, bias=scal(C_BOUT + c)).then_inc(hoc_ready, 1)
            with act.Fori(0, NG) as g:
                act.wait_ge(tail_sum, g * KC + KC)
                go = go_all[:, bass.ds(g, 1), :, :].rearrange("p a c n -> p (a c n)")
                act.activation(go, go, ACT.Tanh).then_inc(tail_tanh, 1)

        @block.vector
        def _(dve):
            done = [0]

            def setup(ins):
                done[0] += 1
                ins.then_inc(setup_link, 1)
                dve.wait_ge(setup_link, done[0])

            dve.wait_ge(small_in_s, 16)
            setup(dve.scalar_tensor_tensor(out=qs[:, 1:2], in0=scal(C_TEMP), scalar=-1.0, in1=scal(C_TEMP), op0=ALU.mult,
                                           op1=ALU.max))
            setup(dve.tensor_scalar(qs[:, 1:2], qs[:, 1:2], 0.1, None, ALU.add))
            setup(dve.reciprocal(qs[:, 2:3], qs[:, 1:2]))
            setup(dve.tensor_scalar(qs[:, 0:1], qs[:, 2:3], 1.0 / math.sqrt(HD), None, ALU.mult))
            setup(dve.memset(qs[:, 3:4], -PI_LOW))
            setup(dve.tensor_scalar(bqs[:, :], small[:, C_BQ:C_BQ + KC], qs[:, 0:1], None, ALU.mult))
            phi = small[:, C_PHI:C_PHI + NP * NF]
            setup(dve.tensor_scalar(turns[:, :], phi, 1 / (2 * math.pi), ROUND, ALU.mult, ALU.add))
            setup(dve.tensor_scalar(turns[:, :], turns[:, :], ROUND, None, ALU.subtract))
            setup(dve.scalar_tensor_tensor(out=phase[:, :], in0=turns[:, :], scalar=-TWO_PI_HI, in1=phi,
                                           op0=ALU.mult, op1=ALU.add))
            setup(dve.scalar_tensor_tensor(out=phase[:, :], in0=turns[:, :], scalar=-TWO_PI_LO, in1=phase[:, :],
                                           op0=ALU.mult, op1=ALU.add))
            dve.tensor_scalar(phase[:, :], phase[:, :], TURN / (2 * math.pi), TURN / 2, ALU.mult,
                              ALU.add).then_inc(setup_dve, 1)
            dve.wait_ge(setup_dve, 1)
            dve.wait_ge(setup_pool, 6)

            def conditioned(g):
                dve.wait_ge(cond_done, g + 1)
                for c in range(KC):
                    bias = wc[:, :, KC * D + c:KC * D + c + 1].to_broadcast([P, GB, L])
                    op = dve.tensor_tensor(by_batch(yT[:, c, :]), by_batch(pf[:, c, :]), bias, ALU.add)
                op.then_inc(y_ready, 1)

            def values(g):
                dve.wait_ge(v_done, g + 1)
                vw = pf[:].rearrange("p c (b k d) -> p (c b) k d", k=NP, d=HD)
                for u in range(2):
                    r = slice(u * L, (u + 1) * L)
                    bias = bv[r, :].rearrange("p (o k d) -> p o k d", o=1, d=HD).to_broadcast([L, GB, NP, HD])
                    op = dve.tensor_tensor(vz[r, :, :, u * HD:(u + 1) * HD], vw[r], bias, ALU.add)
                op.then_inc(v_ready, 1)

            def pair(p):
                return sc[:, p, :, :].rearrange("p b n -> p (b n)")

            def angle(g, p, f):
                if f == 0:
                    if p % PC == 0:
                        dve.wait_ge(s_copied, g * NTILE + TC * (p // PC + 1))
                    wait(dve, score_ready, g * NP + (p - 1))
                dve.tensor_scalar(ang[:, p % 2, f, :], pair(p), TURN / FREQS[f],
                                  phase[:, p * NF + f:p * NF + f + 1], ALU.mult, ALU.add).then_inc(angle_raw, 1)

            def angles(g, p):
                for f in range(NF):
                    angle(g, p, f)

            def wrap(g, p):
                dve.wait_ge(angle_raw, g * (NP * NF) + NF * (p + 1))
                a = ang[:, p % 2, :, :].rearrange("p f n -> p (f n)")
                dve.tensor_scalar(a, a, (1 << TURN_BITS) - 1, None, ALU.bitwise_and).then_inc(angle_ready, 1)

            def next_angles(g, p, k):
                if k < NF:
                    angle(g, p, k)
                else:
                    wrap(g, p)

            def add_sine(g, p, f):
                amp = scal(C_ALPHA + p * NF + f)
                sine = ang[:, p % 2, f, :].bitcast(F32)
                if f == 0:
                    dve.wait_ge(sine_ready, g * NP + (p + 1))
                    dve.tensor_scalar(pair(p), sine, amp, None, ALU.mult).then_inc(score_part, 1)
                    return
                dve.wait_ge(score_part, g * (NP * (NF - 1)) + (p * (NF - 1) + f))
                op = dve.scalar_tensor_tensor(out=pair(p), in0=sine, scalar=amp, in1=pair(p), op0=ALU.mult, op1=ALU.add)
                op.then_inc(score_ready if f == NF - 1 else score_part, 1)

            def divided(g, c):
                n = g * (2 * KC) + 2 * c
                dve.wait_ge(pv_done, g * NP + PC * (c + 1))
                dve.tensor_scalar(rden[:, :], pden[:, :], EPS_W, None, ALU.add).then_inc(att_part, 1)
                dve.wait_ge(att_part, n + 1)
                dve.reciprocal(rden[:, :], rden[:, :]).then_inc(att_part, 1)
                dve.wait_ge(att_part, n + 2)
                dve.tensor_tensor(att[:, c, :], pnum[:, :], rden[:, :], ALU.mult).then_inc(att_ready, 1)
                dve.wait_ge(att_ready, g * KC + (c + 1))

            links = [0]

            def link(g, ins):
                links[0] += 1
                ins.then_inc(rest_link, 1)
                dve.wait_ge(rest_link, g * LINKS + links[0])

            def less_mean(g, n):
                dve.wait_ge(mean_done, g * 2 + (n + 1))
                for c in range(KC):
                    op = dve.tensor_tensor(oT[:, c, :], oT[:, c, :], pr[:, 0, :], ALU.subtract)
                op.then_inc(dev_ready, 1)

            def reciprocal_deviation(g, n):
                dve.wait_ge(dev_ready, g * 2 + (n + 1))
                dve.wait_ge(std_ready, g * 2 + (n + 1))
                link(g, dve.reciprocal(rstd[:, :], rstd[:, :]))

            def residual(g):
                reciprocal_deviation(g, 0)
                dve.wait_ge(xr_loaded, g * 16 + 16)
                for c in range(KC):
                    link(g, dve.scalar_tensor_tensor(out=oT[:, c, :], in0=oT[:, c, :], scalar=scal(C_GAMMA + c),
                                                     in1=rstd[:, :], op0=ALU.mult, op1=ALU.mult))
                for c in range(KC):
                    op = dve.scalar_tensor_tensor(out=x1g[:, c, :], in0=oT[:, c, :], scalar=scal(C_BETA + c),
                                                  in1=xr[:, c, :], op0=ALU.add, op1=ALU.add)
                op.then_inc(x1_ready, 1)

            def hidden(g):
                dve.wait_ge(down_done, g + 1)
                link(g, dve.tensor_tensor(hT[:], by_batch(pr[0:A, 0, :]), w2[:, :, D:D + 1].to_broadcast([A, GB, L]), ALU.add))
                dve.tensor_scalar(hT[:], hT[:], 0.0, None, ALU.max).then_inc(h_ready, 1)

            def of_language(c, k):
                col = KC * A + KC * k + c
                return wa[:, :, col:col + 1].to_broadcast([P, GB, L])

            def adapted(g):
                dve.wait_ge(up_done, g + 1)
                dve.wait_ge(x1_ready, g + 1)
                for c in range(KC):
                    link(g, dve.tensor_tensor(oT[:, c, :], x1g[:, c, :], pr[:, c, :], ALU.add))
                for c in range(KC):
                    op = dve.tensor_tensor(by_batch(oT[:, c, :]), by_batch(oT[:, c, :]), of_language(c, 0), ALU.add)
                op.then_inc(x2_ready, 1)
                dve.wait_ge(x2_ready, g + 1)

            def modulated(g):
                reciprocal_deviation(g, 1)
                for c in range(KC):
                    link(g, dve.tensor_tensor(oT[:, c, :], oT[:, c, :], rstd[:, :], ALU.mult))
                for c in range(KC):
                    link(g, dve.tensor_tensor(by_batch(oT[:, c, :]), by_batch(oT[:, c, :]), of_language(c, 1), ALU.mult))
                for c in range(KC):
                    op = dve.tensor_tensor(by_batch(zT[:, c, :]), by_batch(oT[:, c, :]), of_language(c, 2), ALU.add)
                op.then_inc(z_ready, 1)
                dve.wait_ge(z_ready, g + 1)
                dve.wait_ge(x1_kept, g * 16 + 16)
                dve.sem_inc(rest_free, 1)

            def gate_sum(g, t):
                dve.wait_ge(gate_done, g * GB + (t + 1))
                dve.tensor_tensor(pre[:, :], pgates[t % 2], gate_b[:, :], ALU.add).then_inc(pre_ready, 1)

            def cell_step(g, t):
                dve.wait_ge(gate_ready, g * (2 * GB) + (2 * t + 1))
                dve.tensor_tensor(fc[:, 0, :], gat[:, 0:P], cst[:, :], ALU.mult).then_inc(cell, 1)
                dve.wait_ge(gate_ready, g * (2 * GB) + (2 * t + 2))
                dve.tensor_tensor(fc[:, 1, :], gat[:, P:2 * P], gat[:, 2 * P:3 * P], ALU.mult).then_inc(cell, 1)
                dve.wait_ge(cell, g * (2 * GB) + (2 * t + 2))
                dve.tensor_tensor(cst[:, :], fc[:, 0, :], fc[:, 1, :], ALU.add).then_inc(c_ready, 1)

            def state_copy(g, t):
                dve.wait_ge(ct_done, g * GB + (t + 1))
                dve.tensor_copy(cT[:].rearrange("p c n -> p (c n)"), pct).then_inc(ct_ready, 1)

            conditioned(0)
            angles(0, 0)
            wrap(0, 0)

            def step(i, rest, attention, front):
                r, a, f = i - 1, i, i + 1
                links[0] = 0
                for s in range(REC_SLOT):
                    if attention:
                        angles(a, s + 1)
                        wrap(a, s + 1)
                    if rest and s == 0:
                        divided(r, KC - 1)
                    if rest and s == 1:
                        less_mean(r, 0)
                    if attention and s == 1:
                        values(a)
                    if front and s == 2:
                        conditioned(f)
                    if rest and s == 2:
                        residual(r)
                    if rest and s == 3:
                        adapted(r)
                    if attention and s == 4:
                        divided(a, 0)
                    if attention:
                        for k in range(NF - 1):
                            add_sine(a, s, k)
                    if rest and s == 2:
                        hidden(r)
                    if rest and s == 3:
                        less_mean(r, 1)
                    if rest and s == 4:
                        modulated(r)
                    if attention:
                        add_sine(a, s, NF - 1)
                for n in range(UNITS * (NP - REC_SLOT)):
                    s, k = REC_SLOT + n // UNITS, n % UNITS
                    t, part = n // 4, n % 4
                    if rest and t < GB:
                        if part == 0:
                            gate_sum(r, t)
                        if part == 2:
                            cell_step(r, t)
                        if part == 3:
                            state_copy(r, t)
                    if k <= NF and s + 1 < NP and attention:
                        next_angles(a, s + 1, k)
                    if k <= NF and s + 1 == NP and front:
                        next_angles(f, 0, k)
                    if k > NF and attention:
                        add_sine(a, s, k - NF - 1)
                assert not rest or links[0] == LINKS, links[0]

            rounds(dve, step)
            dve.wait_ge(hoc_ready, KC)
            dve.wait_ge(x1_loaded, 16)
            with dve.Fori(0, NG) as g:
                for c in range(KC):
                    go = go_all[:, bass.ds(g, 1), c, :].rearrange("p a (t n) -> p (a t) n", n=L)
                    dve.tensor_tensor(go, go, hoc[:, c:c + 1, :].to_broadcast([P, GB, L]), ALU.add).then_inc(tail_sum, 1)
                dve.wait_ge(tail_tanh, g + 1)
                go = go_all[:, bass.ds(g, 1), :, :].rearrange("p a c n -> p (a c n)")
                x1 = x1_all[:, bass.ds(g, 1), :].rearrange("p a n -> p (a n)")
                dve.tensor_tensor(go, go, x1, ALU.add).then_inc(tail_out, 1)


_OUT = (NG, P, KC, NT)


def kernel(**inputs):
    import numpy as np
    import concourse.bacc as bacc
    from concourse.bass_utils import run_bass_kernel_spmd

    a = {k: np.asarray(v) for k, v in inputs.items()}

    def chunked(w):
        o, i = w.shape
        return w.T.reshape(i // P, P, o).transpose(1, 0, 2)

    def cols(v):
        return v.reshape(KC, P).T

    x = a["x"].reshape(NG, NT, KC, P).transpose(0, 3, 2, 1)
    ids = np.concatenate([a["itok_B_0_7"], a["itok_B_0_8"]]).reshape(1, 2 * B)
    rows = np.concatenate([a["L0_attn_temperature"], np.full(1, EPS_LN, np.float32)])

    def by_pair(v):
        v = v.reshape(NP, 2, NF).transpose(1, 0, 2).reshape(2, 1, NP * NF)
        return np.broadcast_to(v, (2, L, NP * NF)).reshape(P, NP * NF)

    small = np.concatenate([cols(a["L0_attn_bq"]), cols(a["L0_attn_bk"]), cols(a["L0_attn_bo"]), cols(a["L0_attn_gamma"]),
                            cols(a["L0_attn_beta"]), cols(a["L0_ffn_bo"]), np.broadcast_to(rows, (P, rows.size)),
                            by_pair(a["L0_attn_alpha"]), by_pair(a["L0_attn_phi"])], axis=1)
    cond = a["L0_cond_weight"].transpose(0, 2, 1).reshape(NSUB, KC, P, D).transpose(0, 2, 1, 3).reshape(NSUB, P, KC * D)
    cond = np.concatenate([cond, a["L0_cond_bias"].reshape(NSUB, KC, P).transpose(0, 2, 1)], axis=2)
    down = a["L0_cond2_W1"].reshape(NLANG, KC, P, A).transpose(0, 2, 1, 3).reshape(NLANG, P, KC * A)
    down = np.concatenate([down] + [a["L0_cond2_" + n].reshape(NLANG, KC, P).transpose(0, 2, 1) for n in ("b2", "gamma", "beta")], axis=2)
    up = np.concatenate([a["L0_cond2_W2"], a["L0_cond2_b1"][:, :, None]], axis=2)
    wv = chunked(a["L0_attn_Wv"]).reshape(P, KC, NP, 2, HD).transpose(0, 1, 3, 2, 4).reshape(P, KC, 2, P)
    bv = a["L0_attn_bv"].reshape(NP, 2, HD).transpose(1, 0, 2).reshape(2, 1, P)

    def gate_cols(ws):
        w = np.stack([chunked(w).reshape(P, KC, 2, P) for w in ws], axis=3)
        return w.reshape(P, KC, 2, GATES * P)

    gate_b = np.stack([a["L0_ffn_" + n].reshape(2, P) for n in ("bf", "bi", "bc")], axis=1).reshape(2, 1, GATES * P)
    arrays = {
        "x": x, "ids": ids, "small": small, "cond": cond, "down": down, "up": up,
        "wq": chunked(a["L0_attn_Wq"]), "wk": chunked(a["L0_attn_Wk"]), "wv": wv,
        "bv": np.broadcast_to(bv, (2, L, P)).reshape(P, P), "wo": chunked(a["L0_attn_Wo"]),
        "gate_w": gate_cols([a["L0_ffn_" + n] for n in ("wf", "wi", "wc")]),
        "gate_u": gate_cols([a["L0_ffn_" + n] for n in ("uf", "ui", "uc")]),
        "gate_b": np.broadcast_to(gate_b, (2, L, GATES * P)).reshape(P, GATES * P),
        "c0": np.broadcast_to(a["L0_ffn_in_c"].reshape(2, 1, P), (2, L, P)).reshape(P, P),
        "c0t": np.broadcast_to(cols(a["L0_ffn_in_c"])[:, :, None], (P, KC, L)),
        "wout": chunked(a["L0_ffn_wo"]), "uout": chunked(a["L0_ffn_uo"]), "eye": np.eye(P, dtype=np.float32),
    }
    nc = bacc.Bacc("TRN2", target_bir_lowering=False, num_devices=1)
    feeds, args = {}, []
    for name, v in arrays.items():
        v = np.ascontiguousarray(v)
        feeds[f"in_{name}"] = v
        args.append(nc.dram_tensor(f"in_{name}", v.shape, mybir.dt.from_np(v.dtype), kind="ExternalInput").ap())
    args.append(nc.dram_tensor("out_t", _OUT, F32, kind="ExternalOutput").ap())
    build(nc, *args)
    r = run_bass_kernel_spmd(nc, [feeds], core_ids=[0])
    got = r.results[0]["out_t"]
    return got.transpose(0, 3, 2, 1).reshape(B, L, D)
```
